# Optimizing a Trainium2 kernel written in Bass

```python
import numpy as np
import jax
import jax.numpy as jnp

def _softmax(x, axis=-1):
    return jax.nn.softmax(x, axis=axis)

def _gelu(x):
    return jax.nn.gelu(x, approximate=True)

def _silu(x):
    return jax.nn.silu(x)

def _sigmoid(x):
    return jax.nn.sigmoid(x)

def _layernorm(x, axis=-1, eps=1e-05):
    m = jnp.mean(x, axis=axis, keepdims=True)
    v = jnp.var(x, axis=axis, keepdims=True)
    return (x - m) / jnp.sqrt(v + eps)

def _scatter_add(tgt, idx, src, axis=0):
    return tgt.at[idx].add(src)

def _segment_sum(src, seg, n):
    return jax.ops.segment_sum(src, seg, n)
kernel_name = 'mk_gnn_ffn_d1_gnn_r32_7d39a7'

def setup_inputs(seed: int=0):
    np.random.seed(seed)
    _w = jnp.asarray

    def _rec_inputs():
        import jax
        import jax.numpy as jnp
        _gk = jax.random.key(seed)
        x = -0.0002117 + 1 * jax.random.normal(jax.random.fold_in(_gk, 1), (3125, 256), jnp.float32)
        src = jax.random.randint(jax.random.fold_in(_gk, 2), (50000,), 0, 3125, jnp.int32)
        dst = jax.random.randint(jax.random.fold_in(_gk, 3), (50000,), 0, 3125, jnp.int32)
        _o = jnp.argsort(dst, stable=True)
        src = src[_o]
        dst = dst[_o]
        return (x, src, dst)
    x, src, dst = _rec_inputs()

    def _L0_gnn_setup():
        import jax, jax.numpy as jnp
        import numpy as np
        N_NODES = 3125
        N_EDGES = 100000
        D = 256
        key = jax.random.key(seed)
        ks = jax.random.split(key, 6)
        x = jax.random.normal(ks[0], (N_NODES, D), dtype=jnp.float32)
        edge_src = jax.random.randint(ks[1], (N_EDGES,), 0, N_NODES, dtype=jnp.int32)
        edge_dst = jax.random.randint(ks[2], (N_EDGES,), 0, N_NODES, dtype=jnp.int32)
        w = jnp.ones((1,), dtype=jnp.float32) * 3.0
        W1 = jax.random.normal(ks[3], (64, D), dtype=jnp.float32) * 0.05
        W2 = jax.random.normal(ks[4], (32, 64), dtype=jnp.float32) * 0.1
        W3 = jax.random.normal(ks[5], (D, 32), dtype=jnp.float32) * 0.1
        return {'x': x, 'edge_src': edge_src, 'edge_dst': edge_dst, 'w': w, 'W1': W1, 'W2': W2, 'W3': W3}
    _L0_gnn_all = _L0_gnn_setup()
    _L0_gnn_in = {k: v for k, v in _L0_gnn_all.items() if k in ('w', 'W1', 'W2', 'W3')}
    del _L0_gnn_all

    def _L0_ffn_setup():
        import jax, jax.numpy as jnp
        import numpy as np
        TOP_K = 2
        key = jax.random.key(seed)
        ks = jax.random.split(key, 4)
        B, L, D, H, E = (8, 128, 256, 1024, 8)
        s = 0.02
        return {'x': jax.random.normal(ks[0], (B, L, D), jnp.float32), 'Wg': jax.random.normal(ks[1], (D, E), jnp.float32) * s, 'bg': jnp.zeros((E,), jnp.float32), 'W1': jax.random.normal(ks[2], (E, D, H), jnp.float32) * s, 'b1': jnp.zeros((E, H), jnp.float32), 'W2': jax.random.normal(ks[3], (E, H, D), jnp.float32) * s, 'b2': jnp.zeros((E, D), jnp.float32)}
    _L0_ffn_all = _L0_ffn_setup()
    _L0_ffn_in = {k: v for k, v in _L0_ffn_all.items() if k in ('Wg', 'bg', 'W1', 'b1', 'W2', 'b2')}
    del _L0_ffn_all
    return {'x': x, 'src': src, 'dst': dst, 'L0_gnn_w': _L0_gnn_in['w'], 'L0_gnn_W1': _L0_gnn_in['W1'], 'L0_gnn_W2': _L0_gnn_in['W2'], 'L0_gnn_W3': _L0_gnn_in['W3'], 'L0_ffn_Wg': _L0_ffn_in['Wg'], 'L0_ffn_bg': _L0_ffn_in['bg'], 'L0_ffn_W1': _L0_ffn_in['W1'], 'L0_ffn_b1': _L0_ffn_in['b1'], 'L0_ffn_W2': _L0_ffn_in['W2'], 'L0_ffn_b2': _L0_ffn_in['b2']}

def reference(x, src, dst, L0_gnn_w, L0_gnn_W1, L0_gnn_W2, L0_gnn_W3, L0_ffn_Wg, L0_ffn_bg, L0_ffn_W1, L0_ffn_b1, L0_ffn_W2, L0_ffn_b2):
    import jax
    import jax.numpy as jnp

    def _L0_gnn_ref(x, edge_src, edge_dst, w, W1, W2, W3):
        import jax, jax.numpy as jnp
        import numpy as np
        N_NODES = 3125
        N_EDGES = 100000
        D = 256
        agg = jax.ops.segment_sum(x[edge_dst], edge_src, num_segments=N_NODES)
        y = agg + w * x
        h = jax.nn.relu(jnp.einsum('nd,hd->nh', y, W1))
        h = jax.nn.relu(jnp.einsum('nh,gh->ng', h, W2))
        h = jax.nn.relu(jnp.einsum('ng,og->no', h, W3))
        return h + x

    def _L0_ffn_ref(x, Wg, bg, W1, b1, W2, b2):
        import jax, jax.numpy as jnp
        import numpy as np
        TOP_K = 2
        B, L, D = x.shape
        E = W1.shape[0]
        xf = x.reshape(-1, D)
        gate_logits = xf @ Wg + bg
        top_w, top_i = jax.lax.top_k(gate_logits, TOP_K)
        top_w = jax.nn.softmax(top_w, axis=-1)
        w_dense = jnp.sum(jax.nn.one_hot(top_i, E, dtype=xf.dtype) * top_w[..., None], axis=1)
        out = jnp.zeros_like(xf)
        for e in range(E):
            h = jax.nn.gelu(xf @ W1[e] + b1[e], approximate=False)
            out = out + w_dense[:, e:e + 1] * (h @ W2[e] + b2[e])
        return out.reshape(B, L, D)
    x = x + _L0_gnn_ref(_layernorm(x, axis=-1), src, dst, L0_gnn_w, L0_gnn_W1, L0_gnn_W2, L0_gnn_W3)
    x = x + _L0_ffn_ref(_layernorm(x, axis=-1)[None], L0_ffn_Wg, L0_ffn_bg, L0_ffn_W1, L0_ffn_b1, L0_ffn_W2, L0_ffn_b2)[0]
    return x

_drawn_inputs = setup_inputs


def setup_inputs(seed=0):
    import zlib

    import numpy as np

    out = dict(_drawn_inputs(seed))
    spreads = {'L0_ffn_bg': (0.0, 0.328), 'L0_ffn_b1': (0.0, 0.633), 'L0_ffn_b2': (0.0, 0.1)}
    factors = {}
    for name, (base, spread) in spreads.items():
        noise = np.random.default_rng([zlib.crc32(name.encode()), seed]).standard_normal(out[name].shape)
        drawn = base * np.exp(spread * noise) if base else spread * noise
        out[name] = jnp.asarray(drawn.astype(out[name].dtype))
    for name, factor in factors.items():
        out[name] = (out[name] * factor).astype(out[name].dtype)
    return out
```

```python
from contextlib import ExitStack

import concourse.bass as bass
from concourse import mybir

P = 128
NODES, D, EDGES = 3125, 256, 50000
F1, F2 = 64, 32
EXPERTS, HID, TOPK = 8, 1024, 2
TILES = -(-NODES // P)
ROWS = TILES * P
TAIL = NODES - (TILES - 1) * P
GROUP = 5
GROUPS = TILES // GROUP
UNROLL = 8
EDGE_TILES = -(-EDGES // (P * UNROLL)) * UNROLL
EDGE_LOOPS = EDGE_TILES // UNROLL
HOT_RING = 4
BANK = 512
SLOT_TILES = (TOPK * NODES + EXPERTS * (P - 1)) // P
CHUNK = 1024
CHUNKS = 2 * EXPERTS * D * HID // (P * CHUNK)
HALF = CHUNK // 2
CENTER = NODES // 2
EPS = 1e-5
Z_SCALE, X_SCALE, W_SCALE, H_SCALE = 2.0**5, 2.0**11, 2.0**8, 2.0**4
PADDED_POSITION = 65536.0


def gnn_moe(nc, x, src, dst, w, w1gT, w2gT, w3gT, wg, bg, weights, b1, b2, out):
    fp32, fp16, i32 = mybir.dt.float32, mybir.dt.float16, mybir.dt.int32
    ALU, ACT, AX = mybir.AluOpType, mybir.ActivationFunctionType, mybir.AxisListType

    z_table = nc.dram_tensor("z_table", (ROWS, P), fp16).ap()
    x_table = nc.dram_tensor("x_table", (ROWS, 2 * D), fp16).ap()
    x1_store = nc.dram_tensor("x1_store", (ROWS, D), fp32).ap()
    y_table = nc.dram_tensor("y_table", (TOPK * ROWS + SLOT_TILES * P, D), fp32).ap()

    ctx = ExitStack()
    with ctx:
        def sb(name, shape, dt=fp32):
            return ctx.enter_context(nc.sbuf_tensor(name, shape, dt))

        def sem(name):
            return ctx.enter_context(nc.semaphore(name))

        w_hi = sb("w_hi", [P, CHUNKS * 1024], fp16)
        w_lo = sb("w_lo", [P, CHUNKS * 1024], fp16)
        shared = sb("shared", [P, EXPERTS * HID])
        hot = shared[:, 0:HOT_RING * 1564].bitcast(fp16).rearrange("p (r n) -> p r n", r=HOT_RING)
        node_iota = shared[:, HOT_RING * 1564:HOT_RING * 1564 + 1564].bitcast(fp16)[:, 0:NODES]
        agg_sb = shared[:, 0:ROWS]
        b1_rep = shared[:, :]
        xs = sb("xs", [P, TILES, D])
        z32 = sb("z32", [P, TILES, F1])
        stage = sb("stage", [P, 2, HALF])
        z_rows = sb("z_rows", [P, UNROLL, P], fp16)
        src_i = sb("src_i", [P, EDGE_TILES], i32)
        dst_i = sb("dst_i", [P, EDGE_TILES], i32)
        src_f = src_i[:, :].bitcast(fp32)
        dst_slot = sb("dst_slot", [P, UNROLL], i32)
        spare = w_lo[:, (CHUNKS - 16) * 1024:].bitcast(fp32)
        xn = spare[:, 0:GROUP * D].rearrange("p (j d) -> p j d", j=GROUP)
        xnT = spare[:, GROUP * D:2 * GROUP * D]
        z_tab = spare[:, 2 * GROUP * D:2 * GROUP * D + TILES * F1].bitcast(fp16).rearrange(
            "p (i c) -> p i c", i=TILES)
        hid1T = shared[:, ROWS:ROWS + GROUP * P]
        node_bufs = ROWS + GROUP * P
        xn2T = shared[:, node_bufs:node_bufs + GROUP * D]
        xn2 = shared[:, node_bufs + GROUP * D:node_bufs + 2 * GROUP * D].rearrange("p (j d) -> p j d", j=GROUP)
        xtab = shared[:, node_bufs + 2 * GROUP * D:node_bufs + 3 * GROUP * D].bitcast(fp16).rearrange(
            "p (j c) -> p j c", j=GROUP)
        hid2T = stage[:, :, :].rearrange("p s n -> p (s n)")[:, 0:GROUP * P]
        z_now = stage[:, :, :].rearrange("p s n -> p (s n)")[:, GROUP * P:GROUP * P + GROUP * F1].rearrange(
            "p (j f) -> p j f", j=GROUP)
        w1g = sb("w1g", [P, 2, F1])
        w2g = sb("w2g", [F1, P])
        w3g = sb("w3g", [F2, D])
        wgate = sb("wgate", [P, 2, EXPERTS])
        bg_rep = sb("bg_rep", [P, EXPERTS])
        w_rep = sb("w_rep", [P, 1])
        ident = sb("ident", [P, P])
        ident16 = sb("ident16", [P, P], fp16)
        w_ident = sb("w_ident", [P, P])
        fold = sb("fold", [P, F1])
        zero16 = sb("zero16", [P, P], fp16)
        eps_t = sb("eps_t", [P, 1])
        bn = sb("bn", [P, GROUP, 6])
        mv = sb("mv", [P, GROUP, 2])
        std = sb("std", [P, GROUP])
        rstd = sb("rstd", [P, GROUP])
        nmr = sb("nmr", [P, GROUP])
        xs_flat = xs[:, :, :].rearrange("p i d -> p (i d)")
        TE = TILES * EXPERTS
        used = [0]

        def part(n):
            a = used[0]
            used[0] += n
            return xs_flat[:, a:a + n]

        def te(ap):
            return ap.rearrange("p (i e) -> p i e", e=EXPERTS)

        logits, eq, cand, first1, first2, logits2, both, tmp = (part(TE) for _ in range(8))
        total_em, scan_em, pos_all, tmp2 = (part(TE) for _ in range(4))
        ones_te = part(TE)
        v1, i1, v2, i2, dlt, ex, s1 = (part(TILES) for _ in range(7))
        gate2 = part(TOPK * TILES)
        pos2 = part(TOPK * TILES)
        pos_i = part(TOPK * TILES).bitcast(i32)
        hi_i = part(TOPK * TILES).bitcast(i32)
        lo_i = part(TOPK * TILES).bitcast(i32)
        hi_f, lo_f = part(TOPK * TILES), part(TOPK * TILES)
        tot_e, n_tiles, c_tiles, off_e, off2_e = (part(EXPERTS) for _ in range(5))
        n_int, n_int2 = part(EXPERTS).bitcast(i32), part(EXPERTS).bitcast(i32)
        tile_ge = stage[:, 1, 0:SLOT_TILES * EXPERTS]
        tile_e = part(SLOT_TILES)
        z_flat = z32[:, :, :].rearrange("p i f -> p (i f)")
        lo_hot = z_flat[:, 512:512 + 2 * P].rearrange("p (s n) -> p s n", s=2)
        hi_val = z_flat[:, 768:768 + 4 * SLOT_TILES].rearrange("p (s n) -> p s n", s=2)
        slot_dest1, is_pad, pad_f, tok_f, second = (z_flat[:, 1024 + n * SLOT_TILES:1024 + (n + 1) * SLOT_TILES]
                                                    for n in range(5))
        e_iota = sb("e_iota", [P, EXPERTS])
        valid = sb("valid", [P, TILES])
        pad_pos = sb("pad_pos", [P, TILES])
        rows_flat = z_rows[:, :, :].rearrange("p j c -> p (j c)").bitcast(fp32)
        lo_iota = rows_flat[:, 0:P]
        hi_iota = sb("hi_iota", [P, SLOT_TILES])
        dest_iota = sb("dest_iota", [P, TOPK * TILES])
        trash_iota = sb("trash_iota", [P, SLOT_TILES])
        before = rows_flat[:, P:2 * P]
        ones = rows_flat[:, 2 * P:3 * P]
        slot_dest = sb("slot_dest", [P, SLOT_TILES], i32)
        slot_tok = sb("slot_tok", [P, SLOT_TILES], i32)
        slot_gate = sb("slot_gate", [P, SLOT_TILES])
        tile_expert = sb("tile_expert", [P, SLOT_TILES], i32)
        tok_slot = sb("tok_slot", [P, 1], i32)
        dest_slot = sb("dest_slot", [P, 1], i32)
        b2_rep = xs_flat[:, TILES * D - EXPERTS * D:]
        hb = xs_flat[:, TILES * D - EXPERTS * D - HID:TILES * D - EXPERTS * D]
        assert used[0] <= TILES * D - EXPERTS * D - HID, used
        hid32 = stage[:, :, :].rearrange("p s n -> p (s n)")
        y_a = rows_flat[:, 0:D]
        y_b = rows_flat[:, D:2 * D]
        x_rows = z_flat[:, 0:D].bitcast(fp16)
        xT = z_flat[:, D:2 * D].bitcast(fp16)
        hT_hi = xs_flat[:, 0:HID // 2].bitcast(fp16)
        hT_lo = xs_flat[:, HID // 2:HID].bitcast(fp16)
        fin = w_hi[:, :].bitcast(fp32)
        fx = fin[:, 0:TILES * D].rearrange("p (i d) -> p i d", i=TILES)
        fy0 = fin[:, TILES * D:2 * TILES * D].rearrange("p (i d) -> p i d", i=TILES)
        fy1 = w_lo[:, :].bitcast(fp32)[:, 0:TILES * D].rearrange("p (i d) -> p i d", i=TILES)

        ps = ctx.enter_context(nc.psum_tensor("ps", [P, 8 * BANK], fp32))
        ps_t = ps[:, 0:GROUP * D]
        ps_z = ps[:, 3 * BANK:3 * BANK + GROUP * F1]
        ps_agg = ps[:, 0:NODES]
        ps_u = ps[0:F1, 0:GROUP * P]
        ps_h2 = ps[:, 2 * BANK:2 * BANK + GROUP * P]
        ps_h3 = ps[:, 4 * BANK:4 * BANK + GROUP * D]
        ps_gate = ps[:, 7 * BANK:7 * BANK + TE]
        ps_count = ps[:, 0:2 * TE]
        ps_slot = ps[:, BANK:BANK + 2 * SLOT_TILES]
        ps_hid = ps[:, 0:HID]
        ps_hT = ps[:, 2 * BANK:2 * BANK + HID]
        ps_xT = ps[:, 4 * BANK:4 * BANK + D].bitcast(fp16)
        ps_y = ps[:, 5 * BANK:5 * BANK + D]

        S = {n: sem(n) for n in (
            "z_now_ok const2 x_in params_in edges_in consts zeros const_chain stats aggr std_ok rstd_ok nmr_ok xn_ok "
            "xs_ok xnT_ps xnT_sb z_ps z32_ok z_hi z_lo z_stored src_ok wident_ok idx_copied "
            "hot_ok edge_done w_hi_ok w_lo_ok agg_copied u_ps h1_ok h2_ps h2_ok h3_ps x1_ok "
            "stats2 aggr2 std2_ok rstd2_ok nmr2_ok xn2_ok xn2T_ps xn2T_sb gates_ps x_hi x_lo "
            "x1_stored x_stored chain exp_in exp_ok counts_in counts_ps hot_pair pair_done slots_ps "
            "tables_ok biases_in tok_gathered tok_ps tok_sb hid_ps hb_ok gelu_ok hT_ps hT_hi_ok "
            "hT_lo_ok y_ps y_a_ok y_ok y_scattered tok_idx dest_idx fsum0 fsum out_stored"
        ).split()}
        held = {e.engine: sem(f"held{n}") for n, e in enumerate((nc.gpsimd, nc.vector))}
        z_in = [sem(f"z_in{j}") for j in range(UNROLL)]
        w_in = [sem(f"w_in{s}") for s in range(2)]
        f_in = [sem(f"f_in{g}") for g in range(GROUPS)]

        table_z = z_table.rearrange("(i p) c -> p i c", p=P)
        table_x = x_table.rearrange("(i p) c -> p i c", p=P)
        store_x1 = x1_store.rearrange("(i p) c -> p i c", p=P)
        ysplit = y_table[0:TOPK * ROWS, :].rearrange("(i p) c -> p i c", p=P)
        wflat = weights.rearrange("(q p) n -> q p n", p=P)
        full = TILES - 1
        PARAMS = 8

        def zeros_wide(n):
            return zero16[:, 0:1].broadcast_to([P, n])

        def bcast(ap, n):
            return ap.rearrange("p (o k) -> p o k", o=1).broadcast_to([P, n, ap.shape[1]])

        def bcast_in(ap, n):
            return ap.rearrange("p (k o) -> p k o", o=1).broadcast_to([P, ap.shape[1], n])

        def hold(eng):
            eng.sem_inc(held[eng.engine], 1)

        block = ctx.enter_context(nc.Block())

        @block.sync
        def _(sp):
            sp.dma_start(xs[:, 0:full, :], x[0:full * P, :].rearrange("(i p) d -> p i d", p=P)).then_inc(S["x_in"], 16)
            sp.wait_ge(S["zeros"], 1)
            sp.dma_start(xs[0:TAIL, full, :], x[full * P:NODES, :]).then_inc(S["x_in"], 16)
            sp.dma_start(w1g[:, :, :], w1gT.rearrange("(c p) f -> p c f", p=P)).then_inc(S["params_in"], 16)
            sp.dma_start(w2g[:, 0:F2], w2gT).then_inc(S["params_in"], 16)
            sp.dma_start(w3g[:, :], w3gT).then_inc(S["params_in"], 16)
            sp.dma_start(wgate[:, :, :], wg.rearrange("(c p) e -> p c e", p=P)).then_inc(S["params_in"], 16)
            sp.dma_start(bg_rep[:, :], bg.rearrange("(o e) -> o e", o=1).broadcast_to([P, EXPERTS])).then_inc(S["params_in"], 16)
            sp.dma_start(w_rep[:, :], w.rearrange("(o e) -> o e", o=1).broadcast_to([P, 1])).then_inc(S["params_in"], 16)
            sp.dma_start(src_i[:, :], src).then_inc(S["edges_in"], 16)
            sp.dma_start(dst_i[:, :], dst).then_inc(S["edges_in"], 16)
            with sp.Fori(0, GROUPS) as g:
                sp.wait_ge(S["z_lo"], g + 1)
                sp.dma_start(table_z[:, bass.ds(g * GROUP, GROUP), :],
                             z_tab[:, bass.ds(g * GROUP, GROUP), :]).then_inc(S["z_stored"], 16)
            for s in range(2):
                sp.dma_start(stage[:, s, :], wflat[0, :, s * HALF:(s + 1) * HALF]).then_inc(w_in[s], 16)
            with sp.Fori(1, CHUNKS) as i:
                for s in range(2):
                    sp.wait_ge(S["w_lo_ok"], 2 * i + (s - 1))
                    sp.dma_start(stage[:, s, :], wflat[bass.ds(i, 1), :, s * HALF:(s + 1) * HALF].rearrange(
                        "q p n -> p (q n)")).then_inc(w_in[s], 16)
            with sp.Fori(0, GROUPS) as g:
                sp.wait_ge(S["x_lo"], g + 1)
                sp.dma_start(table_x[:, bass.ds(g * GROUP, GROUP), :], xtab).then_inc(S["x_stored"], 16)
                sp.wait_ge(S["x1_ok"], g + 1)
                sp.dma_start(store_x1[:, bass.ds(g * GROUP, GROUP), :],
                             xs[:, bass.ds(g * GROUP, GROUP), :]).then_inc(S["x1_stored"], 16)
            sp.wait_ge(S["gates_ps"], GROUPS)
            sp.dma_start(b1_rep, b1.rearrange("(o n) -> o n", o=1).broadcast_to([P, EXPERTS * HID])).then_inc(S["biases_in"], 16)
            sp.wait_ge(S["x1_stored"], 16 * GROUPS)
            sp.dma_start(b2_rep, b2.rearrange("(o n) -> o n", o=1).broadcast_to([P, EXPERTS * D])).then_inc(S["biases_in"], 16)
            sp.wait_ge(S["y_scattered"], 16 * SLOT_TILES)
            for g in range(GROUPS):
                last = g == GROUPS - 1
                tiles = slice(g * GROUP, (g + 1) * GROUP - last)
                sp.dma_start(fx[:, tiles, :], store_x1[:, tiles, :]).then_inc(f_in[g], 16)
                sp.dma_start(fy0[:, tiles, :], ysplit[:, tiles, :]).then_inc(f_in[g], 16)
                sp.dma_start(fy1[:, tiles, :], ysplit[:, TILES + tiles.start:TILES + tiles.stop, :]).then_inc(f_in[g], 16)
                if last:
                    sp.dma_start(fx[0:TAIL, full, :], store_x1[0:TAIL, full, :]).then_inc(f_in[g], 16)
                    sp.dma_start(fy0[0:TAIL, full, :], ysplit[0:TAIL, full, :]).then_inc(f_in[g], 16)
                    sp.dma_start(fy1[0:TAIL, full, :], ysplit[0:TAIL, TILES + full, :]).then_inc(f_in[g], 16)
            for g in range(GROUPS):
                last = g == GROUPS - 1
                tiles = slice(g * GROUP, (g + 1) * GROUP - last)
                sp.wait_ge(S["fsum"], g + 1 + last)
                sp.dma_start(out[g * GROUP * P:(tiles.stop) * P, :].rearrange("(i p) d -> p i d", p=P),
                             fx[:, tiles, :]).then_inc(S["out_stored"], 16)
            sp.dma_start(out[full * P:NODES, :], fx[0:TAIL, full, :]).then_inc(S["out_stored"], 16)
            sp.wait_ge(S["out_stored"], 16 * (GROUPS + 1))

        @block.gpsimd
        def _(pool):
            pool.memset(ident[:, :], 0.0).then_inc(S["const_chain"], 1)
            pool.memset(ident16[:, :], 0.0).then_inc(S["const_chain"], 1)
            pool.memset(fold[:, :], 0.0).then_inc(S["const_chain"], 1)
            pool.memset(valid[:, :], 1.0).then_inc(S["const_chain"], 1)
            pool.memset(pad_pos[:, :], 0.0).then_inc(S["const_chain"], 1)
            pool.wait_ge(S["const_chain"], 5)

            def select(ap, op, fill, base, pattern, mult):
                pool.affine_select(out=ap, in_=ap, compare_op=op, fill=fill, base=base,
                                   pattern=pattern, channel_multiplier=mult).then_inc(S["const_chain"], 1)

            select(ident[:, :], ALU.not_equal, 1.0, 0, [[-1, P]], 1)
            select(ident16[:, :], ALU.not_equal, 1.0, 0, [[-1, P]], 1)
            select(fold[:, :], ALU.not_equal, 1.0, 0, [[-1, F1]], 1)
            select(valid[:, full:TILES], ALU.is_gt, 0.0, TAIL, [[0, 1]], -1)
            select(pad_pos[:, full:TILES], ALU.is_gt, PADDED_POSITION, TAIL, [[0, 1]], -1)
            pool.wait_ge(S["const_chain"], 10)
            select(fold[:, :], ALU.not_equal, 1.0, -F1, [[-1, F1]], 1)
            imprecise = dict(allow_small_or_imprecise_dtypes=True)
            for ap, pattern, base, mult in (
                (node_iota, [[1, NODES]], -CENTER, 0),
                (e_iota[:, :], [[1, EXPERTS]], -EXPERTS, 0),
                (hi_iota[:, :], [[1, SLOT_TILES]], 0, 0),
                (dest_iota[:, :], [[ROWS, TOPK], [P, TILES]], 1, 1),
                (trash_iota[:, :], [[P, SLOT_TILES]], TOPK * ROWS + 1, 1),
            ):
                pool.iota(ap, pattern=pattern, base=base, channel_multiplier=mult, **imprecise).then_inc(S["const_chain"], 1)
            pool.wait_ge(S["const_chain"], 16)
            pool.memset(dest_slot[:, :], 0).then_inc(S["consts"], 1)

            pool.wait_ge(S["edges_in"], 32)
            pool.wait_ge(S["z_stored"], 16 * GROUPS)
            with pool.Fori(0, EDGE_LOOPS) as i:
                for j in range(UNROLL):
                    pool.wait_ge(S["idx_copied"], UNROLL * i + (j + 1))
                    hold(pool)
                    pool.indirect_dma_start(
                        out=z_rows[:, j, :], out_offset=None, in_=z_table,
                        in_offset=bass.IndirectOffsetOnAxis(ap=dst_slot[:, j:j + 1], axis=0)).then_inc(z_in[j], 16)

            pool.wait_ge(S["w_lo_ok"], 2 * CHUNKS)
            with pool.Fori(0, GROUPS) as g:
                pool.wait_ge(S["u_ps"], g)
                pool.tensor_copy(z_now[:, :, :], z32[:, bass.ds(g * GROUP, GROUP), :]).then_inc(S["z_now_ok"], 1)
            pool.wait_ge(S["edge_done"], EDGE_TILES + UNROLL + 1)
            pool.memset(ones, 1.0).then_inc(S["const2"], 1)
            pool.memset(before, 1.0).then_inc(S["const2"], 1)
            pool.iota(lo_iota, pattern=[[1, P]], base=0, channel_multiplier=0, **imprecise).then_inc(S["const2"], 1)
            pool.wait_ge(S["const2"], 2)
            pool.affine_select(out=before, in_=before, compare_op=ALU.is_gt, fill=0.0, base=0,
                               pattern=[[1, P]], channel_multiplier=-1).then_inc(S["const2"], 1)

            pool.wait_ge(S["tables_ok"], 1)
            pool.wait_ge(S["x_stored"], 16 * GROUPS)

            def gather(t):
                pool.tensor_copy(tok_slot[:, :], slot_tok[:, bass.ds(t, 1)]).then_inc(S["tok_idx"], 1)
                pool.wait_ge(S["tok_idx"], t + 1)
                hold(pool)
                pool.indirect_dma_start(
                    out=x_rows, out_offset=None, in_=x_table,
                    in_offset=bass.IndirectOffsetOnAxis(ap=tok_slot[:, 0:1], axis=0)).then_inc(S["tok_gathered"], 16)

            def scatter(t):
                pool.wait_ge(S["y_scattered"], 16 * t)
                pool.tensor_copy(dest_slot[:, :], slot_dest[:, bass.ds(t, 1)]).then_inc(S["dest_idx"], 1)
                pool.wait_ge(S["dest_idx"], t + 1)
                pool.wait_ge(S["y_ok"], t + 1)
                hold(pool)
                pool.indirect_dma_start(
                    out=y_table, out_offset=bass.IndirectOffsetOnAxis(ap=dest_slot[:, 0:1], axis=0),
                    in_=y_b, in_offset=None).then_inc(S["y_scattered"], 16)

            gather(0)
            for t in (1, 2):
                pool.wait_ge(S["tok_ps"], t)
                gather(t)
            with pool.Fori(0, SLOT_TILES - 3) as t:
                pool.wait_ge(S["tok_ps"], t + 3)
                gather(t + 3)
                scatter(t)
            for t in range(SLOT_TILES - 3, SLOT_TILES):
                scatter(t)

        @block.vector
        def _(dve):
            dve.memset(xs[:, full:TILES, :], 0.0).then_inc(S["zeros"], 1)
            dve.memset(eps_t[:, :], EPS).then_inc(S["zeros"], 1)
            dve.memset(w2g[:, F2:], 0.0).then_inc(S["zeros"], 1)
            dve.memset(zero16[:, :], 0.0).then_inc(S["zeros"], 1)
            dve.wait_ge(S["edges_in"], 32)
            dve.tensor_scalar(src_f, src_i[:, :], float(-CENTER), None, ALU.add).then_inc(S["src_ok"], 1)
            dve.wait_ge(S["x_in"], 32)

            def stats(g, names):
                n_stats, n_aggr, n_std, n_rstd, n_nmr = names
                for j in range(GROUP):
                    dve.bn_stats(bn[:, j, :], xs[:, bass.ds(g * GROUP + j, 1), :].rearrange(
                        "p i d -> p (i d)")).then_inc(S[n_stats], 1)
                dve.wait_ge(S[n_stats], GROUP * g + GROUP)
                dve.wait_ge(S[n_nmr], g)
                hold(dve)
                for j in range(GROUP):
                    dve.bn_aggr(mv[:, j, :], bn[:, j, :]).then_inc(S[n_aggr], 1)
                dve.wait_ge(S[n_std], g + 1)
                dve.reciprocal(rstd[:, :], std[:, :]).then_inc(S[n_rstd], 1)
                dve.wait_ge(S[n_rstd], g + 1)
                dve.scalar_tensor_tensor(nmr[:, :], mv[:, :, 0], -1.0, rstd[:, :],
                                         ALU.mult, ALU.mult).then_inc(S[n_nmr], 1)

            with dve.Fori(0, GROUPS) as g:
                stats(g, ("stats", "aggr", "std_ok", "rstd_ok", "nmr_ok"))
                group = bass.ds(g * GROUP, GROUP)
                dve.wait_ge(S["xn_ok"], GROUP * g + GROUP)
                dve.tensor_tensor(xs[:, group, :], xs[:, group, :], xn, ALU.add).then_inc(S["xs_ok"], 1)
                dve.wait_ge(S["z_ps"], g + 1)
                pz = ps_z.rearrange("p (j f) -> p j f", f=F1)
                dve.tensor_scalar(z32[:, group, :], pz, Z_SCALE, None, ALU.mult).then_inc(S["z32_ok"], 1)
                dve.tensor_scalar(z_tab[:, group, 0:F1], pz, Z_SCALE, None, ALU.mult).then_inc(S["z_hi"], 1)
                dve.wait_ge(S["z32_ok"], g + 1)
                dve.wait_ge(S["z_hi"], g + 1)
                dve.tensor_tensor(z_tab[:, group, F1:P], z32[:, group, :], z_tab[:, group, 0:F1],
                                  ALU.subtract).then_inc(S["z_lo"], 1)
            dve.wait_ge(S["params_in"], 16 * 6)
            dve.wait_ge(S["consts"], 1)
            dve.tensor_scalar(w_ident[:, :], ident[:, :], w_rep[:, 0:1], None, ALU.mult).then_inc(S["wident_ok"], 1)
            dve.wait_ge(S["src_ok"], 1)
            dve.wait_ge(S["z_stored"], 16 * GROUPS)

            def one_hots(i):
                for j in range(UNROLL):
                    dve.wait_ge(S["edge_done"], UNROLL * i + (j + 1 + UNROLL - HOT_RING))
                    dve.tensor_scalar(hot[:, j % HOT_RING, 0:NODES], node_iota,
                                      src_f[:, bass.ds(i * UNROLL + j, 1)], None,
                                      ALU.is_equal).then_inc(S["hot_ok"], 1)

            with dve.Fori(0, CHUNKS) as i:
                one_hots(i)
                for s in range(2):
                    dve.wait_ge(S["w_hi_ok"], 2 * i + (s + 1))
                    dve.scalar_tensor_tensor(w_lo[:, bass.ds(i * CHUNK + s * HALF, HALF)], stage[:, s, :], W_SCALE,
                                             w_hi[:, bass.ds(i * CHUNK + s * HALF, HALF)],
                                             ALU.mult, ALU.subtract).then_inc(S["w_lo_ok"], 1)
            with dve.Fori(CHUNKS, EDGE_LOOPS) as i:
                one_hots(i)

            half = 3 * BANK
            dve.wait_ge(S["edge_done"], EDGE_TILES + UNROLL + 1)
            dve.memset(agg_sb[:, NODES:ROWS], 0.0).then_inc(S["agg_copied"], 1)
            dve.tensor_copy(agg_sb[:, half:NODES], ps_agg[:, half:NODES]).then_inc(S["agg_copied"], 1)
            with dve.Fori(0, GROUPS) as g:
                group = bass.ds(g * GROUP, GROUP)
                dve.wait_ge(S["h3_ps"], g + 1)
                dve.scalar_tensor_tensor(xs[:, group, :].rearrange("p j d -> p (j d)"), ps_h3, 0.0,
                                         xs[:, group, :].rearrange("p j d -> p (j d)"),
                                         ALU.max, ALU.add).then_inc(S["x1_ok"], 1)
                dve.wait_ge(S["edge_done"], EDGE_TILES + UNROLL + 1)
                dve.wait_ge(S["x1_ok"], g + 1)
                stats(g, ("stats2", "aggr2", "std2_ok", "rstd2_ok", "nmr2_ok"))
                dve.wait_ge(S["x_hi"], g + 1)
                dve.scalar_tensor_tensor(xtab[:, :, D:2 * D], xn2[:, :, :], X_SCALE, xtab[:, :, 0:D],
                                         ALU.mult, ALU.subtract).then_inc(S["x_lo"], 1)

            chain = [0]

            def step(ins):
                chain[0] += 1
                ins.then_inc(S["chain"], 1)
                dve.wait_ge(S["chain"], chain[0])

            dve.wait_ge(S["gates_ps"], GROUPS)
            dve.wait_ge(S["x1_stored"], 16 * GROUPS)
            dve.wait_ge(S["x_lo"], GROUPS)
            dve.wait_ge(S["const2"], 4)
            e_b = bcast(e_iota[:, :], TILES)
            step(dve.tensor_tensor(te(logits), te(ps_gate), bcast(bg_rep[:, :], TILES), ALU.add))

            def first_of(values, v, idx, mask):
                step(dve.tensor_reduce(v, te(values), AX.X, ALU.max))
                step(dve.tensor_tensor(te(eq), te(values), bcast_in(v, EXPERTS), ALU.is_equal))
                step(dve.scalar_tensor_tensor(te(cand), te(eq), -float(EXPERTS), e_b, ALU.mult, ALU.add))
                step(dve.tensor_reduce(idx, te(cand), AX.X, ALU.min))
                step(dve.tensor_scalar(idx, idx, float(EXPERTS), None, ALU.add))
                step(dve.tensor_tensor(te(mask), e_b, bcast_in(idx, EXPERTS), ALU.is_equal))

            first_of(logits, v1, i1, first1)
            step(dve.scalar_tensor_tensor(logits2, first1, -3.0e38, logits, ALU.mult, ALU.add))
            first_of(logits2, v2, i2, first2)
            dve.tensor_tensor(dlt, v2, v1, ALU.subtract).then_inc(S["exp_in"], 1)
            step(dve.tensor_tensor(both, first1, first2, ALU.add))
            dve.tensor_tensor(te(tmp), te(both), bcast_in(valid[:, :], EXPERTS), ALU.mult).then_inc(S["counts_in"], 1)
            step(dve.memset(ones_te, 1.0))
            dve.wait_ge(S["exp_ok"], 1)
            step(dve.tensor_scalar(s1, ex, 1.0, None, ALU.add))
            step(dve.reciprocal(gate2[:, 0:TILES], s1))
            step(dve.tensor_tensor(gate2[:, TILES:], ex, gate2[:, 0:TILES], ALU.mult))
            dve.wait_ge(S["counts_ps"], 1)
            em = lambda ap: ap.rearrange("p (e i) -> p e i", e=EXPERTS)
            step(dve.tensor_copy(em(total_em), ps_count[:, TE:].rearrange("p (i e) -> p e i", e=EXPERTS)))
            step(dve.tensor_tensor_scan(scan_em, ones_te, total_em, 0.0, ALU.mult, ALU.add))
            step(dve.tensor_reduce(tot_e, em(total_em), AX.X, ALU.add))
            step(dve.tensor_tensor(scan_em, scan_em, total_em, ALU.subtract))
            step(dve.tensor_scalar(n_int, tot_e, float(P - 1), None, ALU.add))
            step(dve.tensor_scalar(n_int2, n_int, 7, None, ALU.logical_shift_right))
            step(dve.tensor_copy(n_tiles, n_int2))
            step(dve.tensor_tensor_scan(c_tiles, ones_te[:, 0:EXPERTS], n_tiles, 0.0, ALU.mult, ALU.add))
            step(dve.tensor_tensor(off_e, c_tiles, n_tiles, ALU.subtract))
            step(dve.scalar_tensor_tensor(off2_e, off_e, float(P), em(scan_em)[:, :, 0], ALU.mult, ALU.subtract))
            step(dve.tensor_tensor(te(pos_all), te(ps_count[:, 0:TE]), bcast(off2_e, TILES), ALU.add))
            step(dve.tensor_tensor(te(tmp2), te(pos_all), scan_em.rearrange("p (e i) -> p i e", e=EXPERTS), ALU.add))
            for k, mask in enumerate((first1, first2)):
                pk = pos2[:, k * TILES:(k + 1) * TILES]
                step(dve.tensor_tensor(eq, mask, tmp2, ALU.mult))
                step(dve.tensor_reduce(pk, te(eq), AX.X, ALU.add))
                step(dve.tensor_tensor(pk, pk, pad_pos[:, :], ALU.add))
            step(dve.tensor_copy(pos_i, pos2))
            step(dve.tensor_scalar(hi_i, pos_i, 7, None, ALU.logical_shift_right))
            step(dve.tensor_scalar(lo_i, pos_i, P - 1, None, ALU.bitwise_and))
            step(dve.tensor_copy(hi_f, hi_i))
            step(dve.tensor_copy(lo_f, lo_i))
            tge = tile_ge.rearrange("p (t e) -> p t e", e=EXPERTS)
            step(dve.tensor_tensor(tge, bcast_in(hi_iota[:, :], EXPERTS), bcast(c_tiles, SLOT_TILES), ALU.is_ge))
            step(dve.tensor_reduce(tile_e, tge, AX.X, ALU.add))
            step(dve.tensor_scalar(tile_expert[:, :], tile_e, float(EXPERTS - 1), None, ALU.min))
            with dve.Fori(0, TOPK * TILES // 2) as i:
                for s in range(2):
                    col = bass.ds(2 * i + s, 1)
                    dve.wait_ge(S["pair_done"], 2 * i + (s + 1))
                    dve.tensor_scalar(lo_hot[:, s, :], lo_iota, lo_f[:, col], None, ALU.is_equal).then_inc(S["hot_pair"], 1)
                    dve.tensor_scalar(hi_val[:, s, 0:SLOT_TILES], hi_iota[:, :], hi_f[:, col], dest_iota[:, col],
                                      ALU.is_equal, ALU.mult).then_inc(S["hot_pair"], 1)
                    dve.tensor_scalar(hi_val[:, s, SLOT_TILES:], hi_iota[:, :], hi_f[:, col], gate2[:, col],
                                      ALU.is_equal, ALU.mult).then_inc(S["hot_pair"], 1)
            dve.wait_ge(S["slots_ps"], 1)
            step(dve.tensor_copy(slot_dest1, ps_slot[:, 0:SLOT_TILES]))
            step(dve.tensor_copy(slot_gate[:, :], ps_slot[:, SLOT_TILES:]))
            step(dve.tensor_scalar(is_pad, slot_dest1, 0.5, None, ALU.is_lt))
            step(dve.tensor_tensor(pad_f, is_pad, trash_iota[:, :], ALU.mult))
            step(dve.scalar_tensor_tensor(slot_dest[:, :], slot_dest1, -1.0, pad_f, ALU.add, ALU.add))
            step(dve.tensor_scalar(second, slot_dest1, ROWS + 0.5, float(-ROWS), ALU.is_ge, ALU.mult))
            step(dve.scalar_tensor_tensor(tok_f, slot_dest1, -1.0, second, ALU.add, ALU.add))
            dve.tensor_scalar(slot_tok[:, :], tok_f, 0.0, None, ALU.max).then_inc(S["tables_ok"], 1)

            def copy_xT(t):
                dve.wait_ge(S["tok_ps"], t + 1)
                dve.tensor_copy(xT, ps_xT).then_inc(S["tok_sb"], 1)

            def add_b1(t):
                ex_t = dve.value_load(tile_expert[0:1, bass.ds(t, 1)], min_val=0, max_val=EXPERTS - 1)
                dve.wait_ge(S["hid_ps"], t + 1)
                dve.scalar_tensor_tensor(hb, ps_hid, 1.0 / (X_SCALE * W_SCALE), b1_rep[:, bass.ds(ex_t * HID, HID)],
                                         ALU.mult, ALU.add).then_inc(S["hb_ok"], 1)

            def low_half(t):
                dve.wait_ge(S["hT_hi_ok"], t + 1)
                dve.scalar_tensor_tensor(hT_lo, ps_hT, H_SCALE, hT_hi, ALU.mult, ALU.subtract).then_inc(S["hT_lo_ok"], 1)

            def add_b2(t):
                ex_t = dve.value_load(tile_expert[0:1, bass.ds(t, 1)], min_val=0, max_val=EXPERTS - 1)
                dve.wait_ge(S["y_ps"], t + 1)
                dve.wait_ge(S["y_ok"], t)
                dve.scalar_tensor_tensor(y_a, ps_y, 1.0 / (H_SCALE * W_SCALE), b2_rep[:, bass.ds(ex_t * D, D)],
                                         ALU.mult, ALU.add).then_inc(S["y_a_ok"], 1)

            dve.wait_ge(S["tables_ok"], 1)
            dve.wait_ge(S["biases_in"], 32)
            copy_xT(0)
            add_b1(0)
            copy_xT(1)
            with dve.Fori(0, SLOT_TILES - 2) as t:
                low_half(t)
                add_b1(t + 1)
                copy_xT(t + 2)
                add_b2(t)
            low_half(SLOT_TILES - 2)
            add_b1(SLOT_TILES - 1)
            add_b2(SLOT_TILES - 2)
            low_half(SLOT_TILES - 1)
            add_b2(SLOT_TILES - 1)

            for g in range(GROUPS):
                last = g == GROUPS - 1
                dve.wait_ge(f_in[g], 48 * (1 + last))
                parts = [(slice(0, P), slice(g * GROUP, (g + 1) * GROUP - last))]
                if last:
                    parts.append((slice(0, TAIL), slice(full, TILES)))
                for rows, tiles in parts:
                    dve.tensor_tensor(fy0[rows, tiles, :], fy0[rows, tiles, :], fy1[rows, tiles, :], ALU.add).then_inc(S["fsum0"], 1)
                dve.wait_ge(S["fsum0"], g + 1 + last)
                for rows, tiles in parts:
                    dve.tensor_tensor(fx[rows, tiles, :], fx[rows, tiles, :], fy0[rows, tiles, :], ALU.add).then_inc(S["fsum"], 1)

        @block.scalar
        def _(act):
            act.wait_ge(S["zeros"], 4)

            def normalize(g, target, names):
                n_aggr, n_std, n_nmr, n_xn, free = names
                act.wait_ge(S[n_aggr], GROUP * g + GROUP)
                act.activation(std[:, :], mv[:, :, 1], ACT.Sqrt, bias=eps_t[:, 0:1]).then_inc(S[n_std], 1)
                act.wait_ge(S[n_nmr], g + 1)
                for name in free:
                    act.wait_ge(S[name], g)
                for j in range(GROUP):
                    i = bass.ds(g * GROUP + j, 1)
                    act.activation(target[:, j, :], xs[:, i, :].rearrange("p i d -> p (i d)"), ACT.Identity,
                                   bias=nmr[:, j:j + 1], scale=rstd[:, j:j + 1]).then_inc(S[n_xn], 1)

            with act.Fori(0, GROUPS) as g:
                normalize(g, xn, ("aggr", "std_ok", "nmr_ok", "xn_ok", ("xs_ok", "xnT_ps")))
                act.wait_ge(S["xnT_ps"], g + 1)
                act.wait_ge(S["z_ps"], g)
                act.activation(xnT, ps_t, ACT.Copy).then_inc(S["xnT_sb"], 1)
            act.wait_ge(S["z_stored"], 16 * GROUPS)

            def indices(i):
                for j in range(UNROLL):
                    act.wait_ge(S["edge_done"], UNROLL * i + (j + 1))
                    act.activation(dst_slot[:, j:j + 1], dst_i[:, bass.ds(i * UNROLL + j, 1)],
                                   ACT.Copy).then_inc(S["idx_copied"], 1)

            act.wait_ge(S["edges_in"], 32)
            with act.Fori(0, CHUNKS) as i:
                indices(i)
                for s in range(2):
                    act.wait_ge(w_in[s], 16 * i + 16)
                    act.activation(w_hi[:, bass.ds(i * CHUNK + s * HALF, HALF)], stage[:, s, :], ACT.Copy,
                                   scale=W_SCALE).then_inc(S["w_hi_ok"], 1)
            with act.Fori(CHUNKS, EDGE_LOOPS) as i:
                indices(i)
            half = 3 * BANK
            act.wait_ge(S["edge_done"], EDGE_TILES + UNROLL + 1)
            act.activation(agg_sb[:, 0:half], ps_agg[:, 0:half], ACT.Copy).then_inc(S["agg_copied"], 1)
            with act.Fori(0, GROUPS) as g:
                act.wait_ge(S["u_ps"], g + 1)
                act.wait_ge(S["h2_ps"], g)
                act.activation(hid1T[0:F1, :], ps_u, ACT.Relu, scale=1.0 / Z_SCALE).then_inc(S["h1_ok"], 1)
                act.wait_ge(S["h2_ps"], g + 1)
                act.wait_ge(S["w_lo_ok"], 2 * CHUNKS)
                act.activation(hid2T[0:F2, :], ps_h2[0:F2, :], ACT.Relu).then_inc(S["h2_ok"], 1)
                normalize(g, xn2, ("aggr2", "std2_ok", "nmr2_ok", "xn2_ok", ("x_lo", "xn2T_ps")))
                act.wait_ge(S["xn2_ok"], GROUP * g + GROUP)
                act.wait_ge(S["x_stored"], 16 * g)
                
                act.activation(xtab[:, :, 0:D], xn2[:, :, :], ACT.Copy, scale=X_SCALE).then_inc(S["x_hi"], 1)
                act.wait_ge(S["xn2T_ps"], g + 1)
                act.wait_ge(S["gates_ps"], g)
                act.activation(xn2T, ps_h3, ACT.Copy).then_inc(S["xn2T_sb"], 1)
            act.wait_ge(S["exp_in"], 1)
            act.activation(ex, dlt, ACT.Exp).then_inc(S["exp_ok"], 1)

            def gelu(t):
                act.wait_ge(S["hb_ok"], t + 1)
                act.wait_ge(S["hT_ps"], t)
                act.activation(hid32, hb, ACT.Gelu).then_inc(S["gelu_ok"], 1)

            def high_half(t):
                act.wait_ge(S["hT_ps"], t + 1)
                act.activation(hT_hi, ps_hT, ACT.Copy, scale=H_SCALE).then_inc(S["hT_hi_ok"], 1)

            def weigh(t):
                act.wait_ge(S["y_a_ok"], t + 1)
                act.wait_ge(S["y_scattered"], 16 * t)
                act.activation(y_b, y_a, ACT.Copy, scale=slot_gate[:, bass.ds(t, 1)]).then_inc(S["y_ok"], 1)

            act.wait_ge(S["x_stored"], 16 * GROUPS)
            gelu(0)
            with act.Fori(0, SLOT_TILES - 1) as t:
                high_half(t)
                gelu(t + 1)
                weigh(t)
            high_half(SLOT_TILES - 1)
            weigh(SLOT_TILES - 1)

        @block.tensor
        def _(pe):
            pe.wait_ge(S["params_in"], 16 * 6)
            pe.wait_ge(S["consts"], 1)

            def transposes(target, rows):
                for j in range(GROUP):
                    for c in range(2):
                        last = pe.transpose(target[:, (2 * j + c) * P:(2 * j + c + 1) * P],
                                            rows[:, j, c * P:(c + 1) * P], ident[:, :])
                return last

            with pe.Fori(0, GROUPS) as g:
                pe.wait_ge(S["xn_ok"], GROUP * g + GROUP)
                pe.wait_ge(S["xnT_sb"], g)
                transposes(ps_t, xn).then_inc(S["xnT_ps"], 1)
                pe.wait_ge(S["xnT_sb"], g + 1)
                pe.wait_ge(S["z_hi"], g)
                pe.wait_ge(S["z32_ok"], g)
                for j in range(GROUP):
                    for c in range(2):
                        last = pe.matmul(ps_z[:, j * F1:(j + 1) * F1], xnT[:, (2 * j + c) * P:(2 * j + c + 1) * P],
                                         w1g[:, c, :], start=c == 0, stop=c == 1)
                last.then_inc(S["z_ps"], 1)

            banks = [(a, min(a + BANK, NODES)) for a in range(0, NODES, BANK)]
            pe.wait_ge(S["zeros"], 4)
            pe.wait_ge(S["z_lo"], GROUPS)
            for a, b in banks:
                last = pe.matmul(ps_agg[:, a:b], zero16[:, 0:P], zeros_wide(b - a), start=True, stop=False,
                                 skip_group_check=True)
            last.then_inc(S["edge_done"], UNROLL)
            with pe.Fori(0, EDGE_LOOPS) as i:
                for j in range(UNROLL):
                    pe.wait_ge(z_in[j], 16 * i + 16)
                    pe.wait_ge(S["hot_ok"], UNROLL * i + (j + 1))
                    for a, b in banks:
                        last = pe.matmul(ps_agg[:, a:b], z_rows[:, j, :], hot[:, j % HOT_RING, a:b],
                                         start=False, stop=False, skip_group_check=True)
                    last.then_inc(S["edge_done"], 1)
            for a, b in banks:
                last = pe.matmul(ps_agg[:, a:b], zero16[:, 0:P], zeros_wide(b - a), start=False, stop=True,
                                 skip_group_check=True)
            last.then_inc(S["edge_done"], 1)

            pe.wait_ge(S["wident_ok"], 1)
            pe.wait_ge(S["agg_copied"], 3)
            with pe.Fori(0, GROUPS) as g:
                pe.wait_ge(S["h1_ok"], g)
                pe.wait_ge(S["z_now_ok"], g + 1)
                for j in range(GROUP):
                    pe.matmul(ps_u[:, j * P:(j + 1) * P], fold[:, :], agg_sb[:, bass.ds(g * GROUP * P + j * P, P)],
                              start=True, stop=False)
                    last = pe.matmul(ps_u[:, j * P:(j + 1) * P],
                                     z_now[:, j, :], w_ident[:, :], start=False, stop=True)
                last.then_inc(S["u_ps"], 1)
                pe.wait_ge(S["h1_ok"], g + 1)
                pe.wait_ge(S["h2_ok"], g)
                pe.matmul(ps_h2[:, 0:BANK], w2g[:, :], hid1T[0:F1, 0:BANK], start=True, stop=True)
                pe.matmul(ps_h2[:, BANK:], w2g[:, :], hid1T[0:F1, BANK:], start=True, stop=True).then_inc(S["h2_ps"], 1)
                pe.wait_ge(S["h2_ok"], g + 1)
                pe.wait_ge(S["xn2T_sb"], g)
                for j in range(GROUP):
                    last = pe.matmul(ps_h3[:, j * D:(j + 1) * D], hid2T[0:F2, j * P:(j + 1) * P], w3g[:, :],
                                     start=True, stop=True)
                last.then_inc(S["h3_ps"], 1)
                pe.wait_ge(S["xn2_ok"], GROUP * g + GROUP)
                pe.wait_ge(S["x1_ok"], g + 1)
                transposes(ps_h3, xn2).then_inc(S["xn2T_ps"], 1)
                pe.wait_ge(S["xn2T_sb"], g + 1)
                for j in range(GROUP):
                    for c in range(2):
                        last = pe.matmul(ps_gate[:, bass.ds(g * GROUP * EXPERTS + j * EXPERTS, EXPERTS)],
                                         xn2T[:, (2 * j + c) * P:(2 * j + c + 1) * P], wgate[:, c, :],
                                         start=c == 0, stop=c == 1)
                last.then_inc(S["gates_ps"], 1)

            pe.wait_ge(S["counts_in"], 1)
            pe.wait_ge(S["const2"], 4)
            pe.matmul(ps_count[:, 0:TE], before, tmp, start=True, stop=True)
            pe.matmul(ps_count[:, TE:], ones, tmp, start=True, stop=True).then_inc(S["counts_ps"], 1)
            pe.matmul(ps_slot, zero16[:, 0:P], zeros_wide(2 * SLOT_TILES), start=True, stop=False,
                      skip_group_check=True).then_inc(S["pair_done"], 2)
            with pe.Fori(0, TOPK * TILES // 2) as i:
                for s in range(2):
                    pe.wait_ge(S["hot_pair"], 6 * i + 3 * (s + 1))
                    pe.matmul(ps_slot, lo_hot[:, s, :], hi_val[:, s, :], start=False, stop=False,
                              skip_group_check=True).then_inc(S["pair_done"], 1)
            pe.matmul(ps_slot, zero16[:, 0:P], zeros_wide(2 * SLOT_TILES), start=False, stop=True,
                      skip_group_check=True).then_inc(S["slots_ps"], 1)

            def transpose_tokens(t):
                pe.wait_ge(S["tok_gathered"], 16 * t + 16)
                pe.wait_ge(S["tok_sb"], t)
                for c in range(4):
                    last = pe.transpose(ps_xT[:, c * P:(c + 1) * P], x_rows[:, c * P:(c + 1) * P], ident16[:, :])
                last.then_inc(S["tok_ps"], 1)

            def first_product(t):
                ex_t = pe.value_load(tile_expert[0:1, bass.ds(t, 1)], min_val=0, max_val=EXPERTS - 1)
                pe.wait_ge(S["tok_sb"], t + 1)
                pe.wait_ge(S["hb_ok"], t)
                for half in range(2):
                    o = ps_hid[:, half * BANK:(half + 1) * BANK]
                    for c in range(2):
                        at = bass.ds(ex_t * 2048 + (c * HID + half * BANK), BANK)
                        pe.matmul(o, xT[:, c * P:(c + 1) * P], w_hi[:, at], start=c == 0, stop=False)
                        pe.matmul(o, xT[:, (2 + c) * P:(3 + c) * P], w_hi[:, at], start=False, stop=False)
                        last = pe.matmul(o, xT[:, c * P:(c + 1) * P], w_lo[:, at], start=False, stop=c == 1)
                last.then_inc(S["hid_ps"], 1)

            def transpose_hidden(t):
                pe.wait_ge(S["gelu_ok"], t + 1)
                pe.wait_ge(S["hT_lo_ok"], t)
                for m in range(HID // P):
                    last = pe.transpose(ps_hT[:, m * P:(m + 1) * P], hid32[:, m * P:(m + 1) * P], ident[:, :])
                last.then_inc(S["hT_ps"], 1)

            def second_product(t):
                ex_t = pe.value_load(tile_expert[0:1, bass.ds(t, 1)], min_val=0, max_val=EXPERTS - 1)
                pe.wait_ge(S["hT_lo_ok"], t + 1)
                pe.wait_ge(S["y_a_ok"], t)
                n = HID // P
                for m in range(n):
                    at = bass.ds(ex_t * 2048 + (CHUNKS // 2 * 1024 + m * D), D)
                    pe.matmul(ps_y, hT_hi[:, m * P:(m + 1) * P], w_hi[:, at], start=m == 0, stop=False)
                    pe.matmul(ps_y, hT_lo[:, m * P:(m + 1) * P], w_hi[:, at], start=False, stop=False)
                    last = pe.matmul(ps_y, hT_hi[:, m * P:(m + 1) * P], w_lo[:, at], start=False, stop=m == n - 1)
                last.then_inc(S["y_ps"], 1)

            pe.wait_ge(S["tables_ok"], 1)
            pe.wait_ge(S["w_lo_ok"], 2 * CHUNKS)
            transpose_tokens(0)
            first_product(0)
            transpose_tokens(1)
            with pe.Fori(0, SLOT_TILES - 2) as t:
                transpose_hidden(t)
                first_product(t + 1)
                transpose_tokens(t + 2)
                second_product(t)
            transpose_hidden(SLOT_TILES - 2)
            first_product(SLOT_TILES - 1)
            second_product(SLOT_TILES - 2)
            transpose_hidden(SLOT_TILES - 1)
            second_product(SLOT_TILES - 1)


def kernel(**inputs):
    import numpy as np
    import concourse.bacc as bacc
    from concourse.bass_utils import run_bass_kernel_spmd

    def grab(name):
        return np.ascontiguousarray(np.asarray(inputs[name]))

    def edges(name, fill):
        a = np.full((P * EDGE_TILES,), fill, np.int32)
        a[:EDGES] = grab(name)
        return a.reshape(P, EDGE_TILES)

    arrays = {
        "x": grab("x"),
        "src": edges("src", -1),
        "dst": edges("dst", 0),
        "w": grab("L0_gnn_w"),
        "w1gT": np.ascontiguousarray(grab("L0_gnn_W1").T),
        "w2gT": np.ascontiguousarray(grab("L0_gnn_W2").T),
        "w3gT": np.ascontiguousarray(grab("L0_gnn_W3").T),
        "wg": grab("L0_ffn_Wg"),
        "bg": grab("L0_ffn_bg"),
        "weights": np.concatenate([
            grab("L0_ffn_W1").reshape(-1, 1024),
            grab("L0_ffn_W2").reshape(EXPERTS, 2, 4, P, D).transpose(0, 1, 3, 2, 4).reshape(-1, 1024)]),
        "b1": grab("L0_ffn_b1").reshape(-1),
        "b2": grab("L0_ffn_b2").reshape(-1),
    }
    nc = bacc.Bacc("TRN2", target_bir_lowering=False, num_devices=1)
    args = [nc.dram_tensor(f"in_{n}", a.shape, mybir.dt.from_np(a.dtype), kind="ExternalInput").ap()
            for n, a in arrays.items()]
    out = nc.dram_tensor("out_0", (NODES, D), mybir.dt.float32, kind="ExternalOutput").ap()
    gnn_moe(nc, *args, out)
    r = run_bass_kernel_spmd(nc, [{f"in_{n}": a for n, a in arrays.items()}], core_ids=[0])
    return r.results[0]["out_0"]
```

```python
from contextlib import ExitStack

import concourse.bass as bass
from concourse import mybir

P = 128
NODES, D, EDGES = 3125, 256, 50000
F1, F2 = 64, 32
EXPERTS, HID, TOPK = 8, 1024, 2
TILES = -(-NODES // P)
ROWS = TILES * P
TAIL = NODES - (TILES - 1) * P
GROUP = 5
GROUPS = TILES // GROUP
UNROLL = 8
EDGE_TILES = -(-EDGES // (P * UNROLL)) * UNROLL
EDGE_LOOPS = EDGE_TILES // UNROLL
HOT_RING = 4
WARM_UP = 40
BANK = 512
SLOT_TILES = (TOPK * NODES + EXPERTS * (P - 1)) // P
CHUNK = 1024
CHUNKS = 2 * EXPERTS * D * HID // (P * CHUNK)
HALF = CHUNK // 2
CENTER = NODES // 2
EPS = 1e-5
Z_SCALE, X_SCALE, W_SCALE, H_SCALE = 2.0**5, 2.0**11, 2.0**8, 2.0**4
PADDED_POSITION = 65536.0


def gnn_moe(nc, x, src, dst, w, w1gT, w2gT, w3gT, wg, bg, weights, b1, b2, out):
    fp32, fp16, i32 = mybir.dt.float32, mybir.dt.float16, mybir.dt.int32
    ALU, ACT, AX = mybir.AluOpType, mybir.ActivationFunctionType, mybir.AxisListType

    z_table = nc.dram_tensor("z_table", (ROWS, P), fp16).ap()
    x_table = nc.dram_tensor("x_table", (ROWS + P, 2 * D), fp16).ap()
    total = nc.dram_tensor("total", (ROWS + P, D), fp32).ap()

    ctx = ExitStack()
    with ctx:
        def sb(name, shape, dt=fp32):
            return ctx.enter_context(nc.sbuf_tensor(name, shape, dt))

        def sem(name):
            return ctx.enter_context(nc.semaphore(name))

        w_hi = sb("w_hi", [P, CHUNKS * 1024], fp16)
        w_lo = sb("w_lo", [P, CHUNKS * 1024], fp16)
        shared = sb("shared", [P, EXPERTS * HID])
        hot = shared[:, 0:HOT_RING * 1564].bitcast(fp16).rearrange("p (r n) -> p r n", r=HOT_RING)
        node_iota = shared[:, HOT_RING * 1564:HOT_RING * 1564 + 1564].bitcast(fp16)[:, 0:NODES]
        agg_sb = shared[:, 0:ROWS]
        b1_rep = shared[:, :]
        xs = sb("xs", [P, TILES, D])
        z32 = sb("z32", [P, TILES, F1])
        stage = sb("stage", [P, 2, HALF])
        z_rows = sb("z_rows", [P, UNROLL, P], fp16)
        src_i = sb("src_i", [P, EDGE_TILES], i32)
        dst_i = sb("dst_i", [P, EDGE_TILES], i32)
        src_f = src_i[:, :].bitcast(fp32)
        dst_slot = sb("dst_slot", [P, UNROLL], i32)
        spare = w_lo[:, (CHUNKS - 16) * 1024:].bitcast(fp32)
        xn = spare[:, 0:GROUP * D].rearrange("p (j d) -> p j d", j=GROUP)
        xnT = [spare[:, n * GROUP * D:(n + 1) * GROUP * D].rearrange("p (j d) -> p j d", j=GROUP) for n in (1, 2)]
        z_tab = spare[:, 3 * GROUP * D:3 * GROUP * D + TILES * F1].bitcast(fp16).rearrange(
            "p (i c) -> p i c", i=TILES)
        hid1T = shared[:, ROWS:ROWS + GROUP * P]
        x_tab = shared[:, 0:TILES * D].bitcast(fp16).rearrange("p (i c) -> p i c", i=TILES)
        xn2T = shared[:, TILES * D:(TILES + GROUP) * D].rearrange("p (j d) -> p j d", j=GROUP)
        hid2T = stage[:, :, :].rearrange("p s n -> p (s n)")[:, 0:GROUP * P]
        z_now = stage[:, :, :].rearrange("p s n -> p (s n)")[:, GROUP * P:GROUP * P + GROUP * F1].rearrange(
            "p (j f) -> p j f", j=GROUP)
        w1g = sb("w1g", [P, 2, F1])
        w2g = sb("w2g", [F1, P])
        w3g = sb("w3g", [F2, D])
        wgate = sb("wgate", [P, 2, EXPERTS])
        bg_rep = sb("bg_rep", [P, EXPERTS])
        w_rep = sb("w_rep", [P, 1])
        ident = sb("ident", [P, P])
        ident16 = sb("ident16", [P, P], fp16)
        w_ident = sb("w_ident", [P, P])
        fold = sb("fold", [P, F1])
        zero16 = sb("zero16", [P, P], fp16)
        eps_t = sb("eps_t", [P, 1])
        bn = sb("bn", [P, TILES, 6])
        mv = sb("mv", [P, TILES, 2])
        std = sb("std", [P, TILES])
        rstd = sb("rstd", [P, TILES])
        nmr = sb("nmr", [P, TILES])
        rstd1 = sb("rstd1", [P, TILES])
        xs_flat = xs[:, :, :].rearrange("p i d -> p (i d)")
        TE = TILES * EXPERTS
        used = [0]

        def part(n):
            a = used[0]
            used[0] += n
            return xs_flat[:, a:a + n]

        def te(ap):
            return ap.rearrange("p (i e) -> p i e", e=EXPERTS)

        logits, eq, cand, first1, first2, logits2, both, tmp = (part(TE) for _ in range(8))
        total_em, scan_em, pos_all, tmp2 = (part(TE) for _ in range(4))
        ones_te = part(TE)
        v1, i1, v2, i2, dlt, ex, s1 = (part(TILES) for _ in range(7))
        gate2 = part(TOPK * TILES)
        pos2 = part(TOPK * TILES)
        pos_i = part(TOPK * TILES).bitcast(i32)
        hi_i = part(TOPK * TILES).bitcast(i32)
        lo_i = part(TOPK * TILES).bitcast(i32)
        hi_f, lo_f = part(TOPK * TILES), part(TOPK * TILES)
        tot_e, n_tiles, c_tiles, off_e, off2_e = (part(EXPERTS) for _ in range(5))
        n_int, n_int2 = part(EXPERTS).bitcast(i32), part(EXPERTS).bitcast(i32)
        tile_ge = stage[:, 1, 0:SLOT_TILES * EXPERTS]
        tile_e = part(SLOT_TILES)
        z_flat = z32[:, :, :].rearrange("p i f -> p (i f)")
        SLOT_COLS = 5
        lo_hot, hot_hi, val_hi = (part(2 * SLOT_COLS * n) for n in (P, SLOT_TILES, 2 * SLOT_TILES))
        lo_hot = lo_hot.rearrange("p (s c n) -> p s c n", s=2, c=SLOT_COLS)
        hot_hi = hot_hi.rearrange("p (s c n) -> p s c n", s=2, c=SLOT_COLS)
        val_hi = val_hi.rearrange("p (s c v n) -> p s c v n", s=2, c=SLOT_COLS, v=2)
        slot_row1, is_pad, pad_f = (z_flat[:, 1024 + n * SLOT_TILES:1024 + (n + 1) * SLOT_TILES] for n in range(3))
        e_iota = sb("e_iota", [P, EXPERTS])
        valid = sb("valid", [P, TILES])
        pad_pos = sb("pad_pos", [P, TILES])
        rows_flat = z_rows[:, :, :].rearrange("p j c -> p (j c)").bitcast(fp32)
        lo_iota = rows_flat[:, 0:P]
        hi_iota = sb("hi_iota", [P, SLOT_TILES])
        row_iota = sb("row_iota", [P, TOPK * TILES])
        trash_iota = sb("trash_iota", [P, 1])
        before = rows_flat[:, P:2 * P]
        ones = rows_flat[:, 2 * P:3 * P]
        slot_row = sb("slot_row", [P, SLOT_TILES], i32)
        slot_gate = sb("slot_gate", [P, SLOT_TILES])
        tile_expert = sb("tile_expert", [P, SLOT_TILES], i32)
        tok_slot = sb("tok_slot", [P, 1], i32)
        dest_slot = sb("dest_slot", [P, 1], i32)
        b2_rep = xs_flat[:, TILES * D - EXPERTS * D:]
        hb = xs_flat[:, TILES * D - EXPERTS * D - HID:TILES * D - EXPERTS * D]
        assert used[0] <= TILES * D, used
        hid32 = stage[:, :, :].rearrange("p s n -> p (s n)")
        y_a = rows_flat[:, 0:D]
        y_b = rows_flat[:, D:2 * D]
        x_rows = z_flat[:, 0:D].bitcast(fp16)
        xT = z_flat[:, D:2 * D].bitcast(fp16)
        hT_hi = xs_flat[:, 0:HID // 2].bitcast(fp16)
        hT_lo = xs_flat[:, HID // 2:HID].bitcast(fp16)
        ps = ctx.enter_context(nc.psum_tensor("ps", [P, 8 * BANK], fp32))
        ps_t = [ps[:, j * BANK:j * BANK + D] for j in range(GROUP)]
        ps_z = [ps[:, b * BANK:b * BANK + GROUP * F1] for b in (5, 6)]
        ps_agg = ps[:, 0:NODES]
        ps_u = ps[0:F1, 0:GROUP * P]
        ps_h2 = ps[:, 2 * BANK:2 * BANK + GROUP * P]
        ps_h3 = ps[:, 4 * BANK:4 * BANK + GROUP * D]
        ps_gate = ps[:, 7 * BANK:7 * BANK + TE]
        ps_count = ps[:, 0:2 * TE]
        ps_slot = ps[:, BANK:BANK + 2 * SLOT_TILES]
        ps_hid = ps[:, 0:HID]
        ps_hT = ps[:, 2 * BANK:2 * BANK + HID]
        ps_xT = ps[:, 4 * BANK:4 * BANK + D].bitcast(fp16)
        ps_y = ps[:, 5 * BANK:5 * BANK + D]

        S = {n: sem(n) for n in (
            "z_now_ok const2 rstd1_ok zero_rows params_in edges_in consts zeros const_chain stats aggr std_ok rstd_ok nmr_ok xn_ok "
            "xs_ok xnT_ps xnT_sb z_ps z32_ok z_hi z_lo z_stored src_ok wident_ok idx_copied "
            "hot_ok edge_done w_hi_ok w_lo_ok agg_copied u_ps h1_ok h2_ps h2_ok h3_ps x1_ok "
            "stats2 aggr2 std2_ok rstd2_ok nmr2_ok xn2_ok xn2T_ps xn2T_sb gates_ps x_hi x_lo "
            "x_stored chain exp_in exp_ok counts_in counts_ps lo_hot_ok values_ok hot_hi_ok pair_done slots_ps "
            "tables_ok biases_in biases2_in tok_gathered tok_ps tok_sb hid_ps hb_ok gelu_ok hT_ps hT_hi_ok "
            "hT_lo_ok y_ps y_a_ok y_ok y_scattered tok_idx dest_idx out_stored"
        ).split()}
        held = {e.engine: sem(f"held{n}") for n, e in enumerate((nc.gpsimd, nc.vector))}
        z_in = [sem(f"z_in{j}") for j in range(UNROLL)]
        w_in = [sem(f"w_in{s}") for s in range(2)]
        x_in = [sem(f"x_in{g}") for g in range(GROUPS)]
        x1_stored = [sem(f"x1_stored{g}") for g in range(GROUPS)]

        table_z = z_table.rearrange("(i p) c -> p i c", p=P)
        table_x = x_table.rearrange("(i p) c -> p i c", p=P)
        table_x1 = total.rearrange("(i p) c -> p i c", p=P)
        wflat = weights.rearrange("(q p) n -> q p n", p=P)
        full = TILES - 1
        PARAMS = 8

        def zeros_wide(n):
            return zero16[:, 0:1].broadcast_to([P, n])

        def bcast(ap, n):
            return ap.rearrange("p (o k) -> p o k", o=1).broadcast_to([P, n, ap.shape[1]])

        def bcast_in(ap, n):
            return ap.rearrange("p (k o) -> p k o", o=1).broadcast_to([P, ap.shape[1], n])

        def peeled(eng, n):
            yield 0
            with eng.Fori(1, n) as i:
                yield i

        def freed(eng, name, n):
            if not (isinstance(n, int) and n <= 0):
                eng.wait_ge(S[name], n)

        def hold(eng):
            eng.sem_inc(held[eng.engine], 1)

        block = ctx.enter_context(nc.Block())

        @block.sync
        def _(sp):
            for g in range(GROUPS):
                tiles = slice(g * GROUP, min((g + 1) * GROUP, full))
                sp.dma_start(xs[:, tiles, :], x[tiles.start * P:tiles.stop * P, :].rearrange(
                    "(i p) d -> p i d", p=P)).then_inc(x_in[g], 16)
            sp.wait_ge(S["zeros"], 1)
            sp.dma_start(xs[0:TAIL, full, :], x[full * P:NODES, :]).then_inc(x_in[GROUPS - 1], 16)
            sp.dma_start(w1g[:, :, :], w1gT.rearrange("(c p) f -> p c f", p=P)).then_inc(S["params_in"], 16)
            sp.dma_start(w2g[:, 0:F2], w2gT).then_inc(S["params_in"], 16)
            sp.dma_start(w3g[:, :], w3gT).then_inc(S["params_in"], 16)
            sp.dma_start(wgate[:, :, :], wg.rearrange("(c p) e -> p c e", p=P)).then_inc(S["params_in"], 16)
            sp.dma_start(bg_rep[:, :], bg.rearrange("(o e) -> o e", o=1).broadcast_to([P, EXPERTS])).then_inc(S["params_in"], 16)
            sp.dma_start(w_rep[:, :], w.rearrange("(o e) -> o e", o=1).broadcast_to([P, 1])).then_inc(S["params_in"], 16)
            sp.dma_start(src_i[:, :], src).then_inc(S["edges_in"], 16)
            sp.dma_start(dst_i[:, :], dst).then_inc(S["edges_in"], 16)
            with sp.Fori(0, GROUPS) as g:
                sp.wait_ge(S["z_lo"], g + 1)
                sp.dma_start(table_z[:, bass.ds(g * GROUP, GROUP), :],
                             z_tab[:, bass.ds(g * GROUP, GROUP), :]).then_inc(S["z_stored"], 16)
            for s in range(2):
                sp.dma_start(stage[:, s, :], wflat[0, :, s * HALF:(s + 1) * HALF]).then_inc(w_in[s], 16)
            with sp.Fori(1, CHUNKS) as i:
                for s in range(2):
                    sp.wait_ge(S["w_lo_ok"], 2 * i + (s - 1))
                    sp.dma_start(stage[:, s, :], wflat[bass.ds(i, 1), :, s * HALF:(s + 1) * HALF].rearrange(
                        "q p n -> p (q n)")).then_inc(w_in[s], 16)
            sp.wait_ge(S["zeros"], 4)
            zeros32 = zero16[:, :].bitcast(fp32)
            for table, n in ((x_table.bitcast(fp32), D), (total, D)):
                sp.dma_start(table[ROWS:, :].rearrange("p (a b) -> p a b", b=P // 2),
                             zeros32.rearrange("p (o b) -> p o b", o=1).broadcast_to([P, n * 2 // P, P // 2])
                             ).then_inc(S["zero_rows"], 16)
            for g in range(GROUPS):
                group = slice(g * GROUP, (g + 1) * GROUP)
                sp.wait_ge(S["x1_ok"], g + 1)
                sp.dma_start(table_x1[:, group, :], xs[:, group, :]).then_inc(x1_stored[g], 16)
            with sp.Fori(0, GROUPS) as g:
                sp.wait_ge(S["x_lo"], g + 1)
                sp.dma_start(table_x[:, bass.ds(g * GROUP, GROUP), :],
                             x_tab[:, bass.ds(g * GROUP, GROUP), :]).then_inc(S["x_stored"], 16)
            sp.wait_ge(S["gates_ps"], GROUPS)
            sp.wait_ge(S["x_stored"], 16 * GROUPS)
            sp.dma_start(b1_rep, b1.rearrange("(o n) -> o n", o=1).broadcast_to([P, EXPERTS * HID])).then_inc(S["biases_in"], 16)
            sp.wait_ge(S["slots_ps"], 1)
            sp.dma_start(b2_rep, b2.rearrange("(o n) -> o n", o=1).broadcast_to([P, EXPERTS * D])).then_inc(S["biases2_in"], 16)
            sp.wait_ge(S["y_scattered"], 16 * SLOT_TILES)
            sp.dma_start(out.rearrange("n d -> (n d)").rearrange("(k m) -> k m", k=P),
                         total[0:NODES, :].rearrange("n d -> (n d)").rearrange("(k m) -> k m", k=P)
                         ).then_inc(S["out_stored"], 16)
            sp.wait_ge(S["out_stored"], 16)

        @block.gpsimd
        def _(pool):
            pool.memset(ident[:, :], 0.0).then_inc(S["const_chain"], 1)
            pool.memset(ident16[:, :], 0.0).then_inc(S["const_chain"], 1)
            pool.memset(fold[:, :], 0.0).then_inc(S["const_chain"], 1)
            pool.memset(valid[:, :], 1.0).then_inc(S["const_chain"], 1)
            pool.memset(pad_pos[:, :], 0.0).then_inc(S["const_chain"], 1)
            pool.wait_ge(S["const_chain"], 5)

            def select(ap, op, fill, base, pattern, mult):
                pool.affine_select(out=ap, in_=ap, compare_op=op, fill=fill, base=base,
                                   pattern=pattern, channel_multiplier=mult).then_inc(S["const_chain"], 1)

            select(ident[:, :], ALU.not_equal, 1.0, 0, [[-1, P]], 1)
            select(ident16[:, :], ALU.not_equal, 1.0, 0, [[-1, P]], 1)
            select(fold[:, :], ALU.not_equal, 1.0, 0, [[-1, F1]], 1)
            select(valid[:, full:TILES], ALU.is_gt, 0.0, TAIL, [[0, 1]], -1)
            select(pad_pos[:, full:TILES], ALU.is_gt, PADDED_POSITION, TAIL, [[0, 1]], -1)
            pool.wait_ge(S["const_chain"], 10)
            select(fold[:, :], ALU.not_equal, 1.0, -F1, [[-1, F1]], 1)
            imprecise = dict(allow_small_or_imprecise_dtypes=True)
            for ap, pattern, base, mult in (
                (node_iota, [[1, NODES]], -CENTER, 0),
                (e_iota[:, :], [[1, EXPERTS]], -EXPERTS, 0),
                (hi_iota[:, :], [[1, SLOT_TILES]], 0, 0),
                (row_iota[:, :], [[0, TOPK], [P, TILES]], 1, 1),
                (trash_iota[:, :], [[0, 1]], ROWS + 1, 1),
            ):
                pool.iota(ap, pattern=pattern, base=base, channel_multiplier=mult, **imprecise).then_inc(S["const_chain"], 1)
            pool.wait_ge(S["const_chain"], 16)
            pool.memset(dest_slot[:, :], 0).then_inc(S["consts"], 1)

            pool.wait_ge(S["edges_in"], 32)
            pool.wait_ge(S["z_stored"], 16 * GROUPS)
            with pool.Fori(0, EDGE_LOOPS) as i:
                for j in range(UNROLL):
                    pool.wait_ge(S["idx_copied"], UNROLL * i + (j + 1))
                    hold(pool)
                    pool.indirect_dma_start(
                        out=z_rows[:, j, :], out_offset=None, in_=z_table,
                        in_offset=bass.IndirectOffsetOnAxis(ap=dst_slot[:, j:j + 1], axis=0)).then_inc(z_in[j], 16)

            pool.wait_ge(S["w_lo_ok"], 2 * CHUNKS)
            for g in peeled(pool, GROUPS):
                freed(pool, "u_ps", g)
                pool.tensor_copy(z_now[:, :, :], z32[:, bass.ds(g * GROUP, GROUP), :]).then_inc(S["z_now_ok"], 1)
            pool.wait_ge(S["edge_done"], EDGE_TILES + UNROLL + 1)
            pool.memset(ones, 1.0).then_inc(S["const2"], 1)
            pool.memset(before, 1.0).then_inc(S["const2"], 1)
            pool.iota(lo_iota, pattern=[[1, P]], base=0, channel_multiplier=0, **imprecise).then_inc(S["const2"], 1)
            pool.wait_ge(S["const2"], 2)
            pool.affine_select(out=before, in_=before, compare_op=ALU.is_gt, fill=0.0, base=0,
                               pattern=[[1, P]], channel_multiplier=-1).then_inc(S["const2"], 1)

            with pool.Fori(0, TOPK * TILES // (2 * SLOT_COLS)) as i:
                for s in range(2):
                    cols = bass.ds(i * (2 * SLOT_COLS) + s * SLOT_COLS, SLOT_COLS)
                    pool.wait_ge(S["hot_hi_ok"], 2 * i + (s + 1))
                    for v, values in enumerate((row_iota, gate2)):
                        pool.tensor_tensor(val_hi[:, s, :, v, :], hot_hi[:, s], bcast_in(values[:, cols], SLOT_TILES),
                                           ALU.mult).then_inc(S["values_ok"], 1)

            pool.wait_ge(S["tables_ok"], 1)
            pool.wait_ge(S["x_stored"], 16 * GROUPS)
            pool.wait_ge(S["zero_rows"], 32)

            def gather(t):
                pool.tensor_copy(tok_slot[:, :], slot_row[:, bass.ds(t, 1)]).then_inc(S["tok_idx"], 1)
                pool.wait_ge(S["tok_idx"], t + 1)
                hold(pool)
                pool.indirect_dma_start(
                    out=x_rows, out_offset=None, in_=x_table,
                    in_offset=bass.IndirectOffsetOnAxis(ap=tok_slot[:, 0:1], axis=0)).then_inc(S["tok_gathered"], 16)

            def scatter(t):
                freed(pool, "y_scattered", 16 * t)
                pool.tensor_copy(dest_slot[:, :], slot_row[:, bass.ds(t, 1)]).then_inc(S["dest_idx"], 1)
                pool.wait_ge(S["dest_idx"], t + 1)
                pool.wait_ge(S["y_ok"], t + 1)
                hold(pool)
                pool.indirect_dma_start(
                    out=total, out_offset=bass.IndirectOffsetOnAxis(ap=dest_slot[:, 0:1], axis=0),
                    in_=y_b, in_offset=None, compute_op=ALU.add).then_inc(S["y_scattered"], 16)

            gather(0)
            for t in (1, 2):
                pool.wait_ge(S["tok_ps"], t)
                gather(t)
            for t in peeled(pool, SLOT_TILES - 3):
                pool.wait_ge(S["tok_ps"], t + 3)
                gather(t + 3)
                scatter(t)
            for t in range(SLOT_TILES - 3, SLOT_TILES):
                scatter(t)

        @block.vector
        def _(dve):
            dve.memset(xs[:, full:TILES, :], 0.0).then_inc(S["zeros"], 1)
            dve.memset(eps_t[:, :], EPS).then_inc(S["zeros"], 1)
            dve.memset(w2g[:, F2:], 0.0).then_inc(S["zeros"], 1)
            dve.memset(zero16[:, :], 0.0).then_inc(S["zeros"], 1)

            def stats(g, names):
                n_stats, n_aggr = names
                for i in range(g * GROUP, (g + 1) * GROUP):
                    dve.bn_stats(bn[:, i, :], xs[:, i, :]).then_inc(S[n_stats], 1)
                dve.wait_ge(S[n_stats], (g + 1) * GROUP)
                for i in range(g * GROUP, (g + 1) * GROUP):
                    dve.bn_aggr(mv[:, i, :], bn[:, i, :]).then_inc(S[n_aggr], 1)

            def scales(n_std, n_rstd, n_nmr):
                dve.wait_ge(S[n_std], 1)
                dve.reciprocal(rstd[:, :], std[:, :]).then_inc(S[n_rstd], 1)
                dve.wait_ge(S[n_rstd], 1)
                dve.scalar_tensor_tensor(nmr[:, :], mv[:, :, 0], -1.0, rstd[:, :],
                                         ALU.mult, ALU.mult).then_inc(S[n_nmr], 1)
                dve.wait_ge(S[n_nmr], 1)

            def normalize(g):
                for j in range(GROUP):
                    i = bass.ds(g * GROUP + j, 1)
                    freed(dve, "xnT_ps", GROUP * g + (j + 1 - GROUP))
                    dve.tensor_scalar(xn[:, j, :], xs[:, i, :].rearrange("p i d -> p (i d)"),
                                      rstd[:, i], nmr[:, i], ALU.mult, ALU.add).then_inc(S["xn_ok"], 1)

            for g in range(GROUPS):
                dve.wait_ge(x_in[g], 32 if g == GROUPS - 1 else 16)
                stats(g, ("stats", "aggr"))
            scales("std_ok", "rstd_ok", "nmr_ok")
            dve.tensor_scalar(rstd1[:, :], rstd[:, :], 1.0, None, ALU.add).then_inc(S["rstd1_ok"], 1)

            def z_halves(g):
                group = slice(g * GROUP, (g + 1) * GROUP)
                dve.wait_ge(S["z_ps"], g + 1)
                pz = ps_z[g % 2].rearrange("p (j f) -> p j f", f=F1)
                dve.tensor_scalar(z32[:, group, :], pz, Z_SCALE, None, ALU.mult).then_inc(S["z32_ok"], 1)
                dve.tensor_scalar(z_tab[:, group, 0:F1], pz, Z_SCALE, None, ALU.mult).then_inc(S["z_hi"], 1)
                dve.wait_ge(S["z32_ok"], g + 1)
                dve.wait_ge(S["z_hi"], g + 1)
                dve.tensor_tensor(z_tab[:, group, F1:P], z32[:, group, :], z_tab[:, group, 0:F1],
                                  ALU.subtract).then_inc(S["z_lo"], 1)

            normalize(0)
            normalize(1)
            for g in range(GROUPS - 2):
                normalize(g + 2)
                z_halves(g)
            z_halves(GROUPS - 2)
            z_halves(GROUPS - 1)
            dve.wait_ge(S["params_in"], 16 * 6)
            dve.wait_ge(S["consts"], 1)
            dve.tensor_scalar(w_ident[:, :], ident[:, :], w_rep[:, 0:1], None, ALU.mult).then_inc(S["wident_ok"], 1)
            dve.wait_ge(S["edges_in"], 32)
            dve.tensor_scalar(src_f, src_i[:, :], float(-CENTER), None, ALU.add).then_inc(S["src_ok"], 1)
            dve.wait_ge(S["src_ok"], 1)
            dve.wait_ge(S["z_stored"], 16 * GROUPS)

            def one_hots(i):
                for j in range(UNROLL):
                    dve.wait_ge(S["edge_done"], UNROLL * i + (j + 1 + UNROLL - HOT_RING))
                    dve.tensor_scalar(hot[:, j % HOT_RING, 0:NODES], node_iota,
                                      src_f[:, bass.ds(i * UNROLL + j, 1)], None,
                                      ALU.is_equal).then_inc(S["hot_ok"], 1)

            with dve.Fori(0, CHUNKS) as i:
                one_hots(i)
                for s in range(2):
                    dve.wait_ge(S["w_hi_ok"], 2 * i + (s + 1))
                    dve.scalar_tensor_tensor(w_lo[:, bass.ds(i * CHUNK + s * HALF, HALF)], stage[:, s, :], W_SCALE,
                                             w_hi[:, bass.ds(i * CHUNK + s * HALF, HALF)],
                                             ALU.mult, ALU.subtract).then_inc(S["w_lo_ok"], 1)
            with dve.Fori(CHUNKS, EDGE_LOOPS) as i:
                one_hots(i)

            half = 3 * BANK
            dve.wait_ge(S["edge_done"], EDGE_TILES + UNROLL + 1)
            dve.memset(agg_sb[:, NODES:ROWS], 0.0).then_inc(S["agg_copied"], 1)
            dve.tensor_copy(agg_sb[:, half:NODES], ps_agg[:, half:NODES]).then_inc(S["agg_copied"], 1)
            dve.wait_ge(S["xs_ok"], TILES)
            for g in range(GROUPS):
                group = slice(g * GROUP, (g + 1) * GROUP)
                dve.wait_ge(S["h3_ps"], g + 1)
                dve.scalar_tensor_tensor(xs[:, group, :].rearrange("p j d -> p (j d)"), ps_h3, 0.0,
                                         xs[:, group, :].rearrange("p j d -> p (j d)"),
                                         ALU.max, ALU.add).then_inc(S["x1_ok"], 1)
                dve.wait_ge(S["x1_ok"], g + 1)
                stats(g, ("stats2", "aggr2"))
            scales("std2_ok", "rstd2_ok", "nmr2_ok")

            def x_low(g):
                group = slice(g * GROUP, (g + 1) * GROUP)
                dve.wait_ge(S["x_hi"], g + 1)
                dve.scalar_tensor_tensor(x_tab[:, group, D:2 * D], xs[:, group, :], X_SCALE, x_tab[:, group, 0:D],
                                         ALU.mult, ALU.subtract).then_inc(S["x_lo"], 1)

            for g in range(GROUPS):
                dve.wait_ge(x1_stored[g], 16)
                for i in range(g * GROUP, (g + 1) * GROUP):
                    dve.tensor_scalar(xs[:, i, :], xs[:, i, :], rstd[:, i:i + 1], nmr[:, i:i + 1],
                                      ALU.mult, ALU.add).then_inc(S["xn2_ok"], 1)
                if g > 0:
                    x_low(g - 1)
            x_low(GROUPS - 1)

            chain = [0]

            def step(ins):
                chain[0] += 1
                ins.then_inc(S["chain"], 1)
                dve.wait_ge(S["chain"], chain[0])

            dve.wait_ge(S["gates_ps"], GROUPS)
            dve.wait_ge(S["x_lo"], GROUPS)
            dve.wait_ge(S["const2"], 4)
            e_b = bcast(e_iota[:, :], TILES)
            step(dve.tensor_tensor(te(logits), te(ps_gate), bcast(bg_rep[:, :], TILES), ALU.add))

            def first_of(values, v, idx, mask):
                step(dve.tensor_reduce(v, te(values), AX.X, ALU.max))
                step(dve.tensor_tensor(te(eq), te(values), bcast_in(v, EXPERTS), ALU.is_equal))
                step(dve.scalar_tensor_tensor(te(cand), te(eq), -float(EXPERTS), e_b, ALU.mult, ALU.add))
                step(dve.tensor_reduce(idx, te(cand), AX.X, ALU.min))
                step(dve.tensor_scalar(idx, idx, float(EXPERTS), None, ALU.add))
                step(dve.tensor_tensor(te(mask), e_b, bcast_in(idx, EXPERTS), ALU.is_equal))

            first_of(logits, v1, i1, first1)
            step(dve.scalar_tensor_tensor(logits2, first1, -3.0e38, logits, ALU.mult, ALU.add))
            first_of(logits2, v2, i2, first2)
            dve.tensor_tensor(dlt, v2, v1, ALU.subtract).then_inc(S["exp_in"], 1)
            step(dve.tensor_tensor(both, first1, first2, ALU.add))
            dve.tensor_tensor(te(tmp), te(both), bcast_in(valid[:, :], EXPERTS), ALU.mult).then_inc(S["counts_in"], 1)
            step(dve.memset(ones_te, 1.0))
            dve.wait_ge(S["exp_ok"], 1)
            step(dve.tensor_scalar(s1, ex, 1.0, None, ALU.add))
            step(dve.reciprocal(gate2[:, 0:TILES], s1))
            step(dve.tensor_tensor(gate2[:, TILES:], ex, gate2[:, 0:TILES], ALU.mult))
            dve.wait_ge(S["counts_ps"], 1)
            em = lambda ap: ap.rearrange("p (e i) -> p e i", e=EXPERTS)
            step(dve.tensor_copy(em(total_em), ps_count[:, TE:].rearrange("p (i e) -> p e i", e=EXPERTS)))
            step(dve.tensor_tensor_scan(scan_em, ones_te, total_em, 0.0, ALU.mult, ALU.add))
            step(dve.tensor_reduce(tot_e, em(total_em), AX.X, ALU.add))
            step(dve.tensor_tensor(scan_em, scan_em, total_em, ALU.subtract))
            step(dve.tensor_scalar(n_int, tot_e, float(P - 1), None, ALU.add))
            step(dve.tensor_scalar(n_int2, n_int, 7, None, ALU.logical_shift_right))
            step(dve.tensor_copy(n_tiles, n_int2))
            step(dve.tensor_tensor_scan(c_tiles, ones_te[:, 0:EXPERTS], n_tiles, 0.0, ALU.mult, ALU.add))
            step(dve.tensor_tensor(off_e, c_tiles, n_tiles, ALU.subtract))
            step(dve.scalar_tensor_tensor(off2_e, off_e, float(P), em(scan_em)[:, :, 0], ALU.mult, ALU.subtract))
            step(dve.tensor_tensor(te(pos_all), te(ps_count[:, 0:TE]), bcast(off2_e, TILES), ALU.add))
            step(dve.tensor_tensor(te(tmp2), te(pos_all), scan_em.rearrange("p (e i) -> p i e", e=EXPERTS), ALU.add))
            for k, mask in enumerate((first1, first2)):
                pk = pos2[:, k * TILES:(k + 1) * TILES]
                step(dve.tensor_tensor(eq, mask, tmp2, ALU.mult))
                step(dve.tensor_reduce(pk, te(eq), AX.X, ALU.add))
                step(dve.tensor_tensor(pk, pk, pad_pos[:, :], ALU.add))
            step(dve.tensor_copy(pos_i, pos2))
            step(dve.tensor_scalar(hi_i, pos_i, 7, None, ALU.logical_shift_right))
            step(dve.tensor_scalar(lo_i, pos_i, P - 1, None, ALU.bitwise_and))
            step(dve.tensor_copy(hi_f, hi_i))
            step(dve.tensor_copy(lo_f, lo_i))
            tge = tile_ge.rearrange("p (t e) -> p t e", e=EXPERTS)
            step(dve.tensor_tensor(tge, bcast_in(hi_iota[:, :], EXPERTS), bcast(c_tiles, SLOT_TILES), ALU.is_ge))
            step(dve.tensor_reduce(tile_e, tge, AX.X, ALU.add))
            step(dve.tensor_scalar(tile_expert[:, :], tile_e, float(EXPERTS - 1), None, ALU.min))
            with dve.Fori(0, TOPK * TILES // (2 * SLOT_COLS)) as i:
                for s in range(2):
                    cols = bass.ds(i * (2 * SLOT_COLS) + s * SLOT_COLS, SLOT_COLS)
                    dve.wait_ge(S["pair_done"], 2 * i + (s + 1))
                    dve.tensor_tensor(hot_hi[:, s], bcast(hi_iota[:, :], SLOT_COLS),
                                      bcast_in(hi_f[:, cols], SLOT_TILES), ALU.is_equal).then_inc(S["hot_hi_ok"], 1)
                    dve.tensor_tensor(lo_hot[:, s], bcast(lo_iota, SLOT_COLS), bcast_in(lo_f[:, cols], P),
                                      ALU.is_equal).then_inc(S["lo_hot_ok"], 1)
            dve.wait_ge(S["slots_ps"], 1)
            step(dve.tensor_copy(slot_row1, ps_slot[:, 0:SLOT_TILES]))
            step(dve.tensor_copy(slot_gate[:, :], ps_slot[:, SLOT_TILES:]))
            step(dve.tensor_scalar(is_pad, slot_row1, 0.5, None, ALU.is_lt))
            step(dve.tensor_scalar(pad_f, is_pad, trash_iota[:, 0:1], -1.0, ALU.mult, ALU.add))
            dve.tensor_tensor(slot_row[:, :], slot_row1, pad_f, ALU.add).then_inc(S["tables_ok"], 1)

            def copy_xT(t):
                dve.wait_ge(S["tok_ps"], t + 1)
                dve.tensor_copy(xT, ps_xT).then_inc(S["tok_sb"], 1)

            def add_b1(t):
                ex_t = dve.value_load(tile_expert[0:1, bass.ds(t, 1)], min_val=0, max_val=EXPERTS - 1)
                dve.wait_ge(S["hid_ps"], t + 1)
                dve.scalar_tensor_tensor(hb, ps_hid, 1.0 / (X_SCALE * W_SCALE), b1_rep[:, bass.ds(ex_t * HID, HID)],
                                         ALU.mult, ALU.add).then_inc(S["hb_ok"], 1)

            def low_half(t):
                dve.wait_ge(S["hT_hi_ok"], t + 1)
                dve.scalar_tensor_tensor(hT_lo, ps_hT, H_SCALE, hT_hi, ALU.mult, ALU.subtract).then_inc(S["hT_lo_ok"], 1)

            def add_b2(t):
                ex_t = dve.value_load(tile_expert[0:1, bass.ds(t, 1)], min_val=0, max_val=EXPERTS - 1)
                dve.wait_ge(S["y_ps"], t + 1)
                freed(dve, "y_ok", t)
                dve.scalar_tensor_tensor(y_a, ps_y, 1.0 / (H_SCALE * W_SCALE), b2_rep[:, bass.ds(ex_t * D, D)],
                                         ALU.mult, ALU.add).then_inc(S["y_a_ok"], 1)

            dve.wait_ge(S["tables_ok"], 1)
            dve.wait_ge(S["biases_in"], 16)
            copy_xT(0)
            add_b1(0)
            copy_xT(1)
            dve.wait_ge(S["biases2_in"], 16)
            for t in peeled(dve, SLOT_TILES - 2):
                low_half(t)
                add_b1(t + 1)
                copy_xT(t + 2)
                add_b2(t)
            low_half(SLOT_TILES - 2)
            add_b1(SLOT_TILES - 1)
            add_b2(SLOT_TILES - 2)
            low_half(SLOT_TILES - 1)
            add_b2(SLOT_TILES - 1)

        @block.scalar
        def _(act):
            act.wait_ge(S["zeros"], 4)

            act.wait_ge(S["aggr"], TILES)
            act.activation(std[:, :], mv[:, :, 1], ACT.Sqrt, bias=eps_t[:, 0:1]).then_inc(S["std_ok"], 1)

            def copy_transposed(g, target, names, buffers=1):
                n_ps, n_sb, n_free = names
                freed(act, n_free, g + 1 - buffers)
                for j in range(GROUP):
                    act.wait_ge(S[n_ps], GROUP * g + (j + 1))
                    act.activation(target[:, j, :], ps_t[j], ACT.Copy).then_inc(S[n_sb], 1)

            for g in range(GROUPS):
                copy_transposed(g, xnT[g % 2], ("xnT_ps", "xnT_sb", "z_ps"), 2)
            act.wait_ge(S["z_stored"], 16 * GROUPS)

            def indices(i):
                for j in range(UNROLL):
                    act.wait_ge(S["edge_done"], UNROLL * i + (j + 1))
                    act.activation(dst_slot[:, j:j + 1], dst_i[:, bass.ds(i * UNROLL + j, 1)],
                                   ACT.Copy).then_inc(S["idx_copied"], 1)

            act.wait_ge(S["edges_in"], 32)
            act.wait_ge(S["rstd1_ok"], 1)
            with act.Fori(0, CHUNKS) as i:
                indices(i)
                for s in range(2):
                    act.wait_ge(w_in[s], 16 * i + 16)
                    act.activation(w_hi[:, bass.ds(i * CHUNK + s * HALF, HALF)], stage[:, s, :], ACT.Copy,
                                   scale=W_SCALE).then_inc(S["w_hi_ok"], 1)
            with act.Fori(CHUNKS, CHUNKS + GROUPS) as i:
                indices(i)
                for j in range(GROUP):
                    at = bass.ds((i - CHUNKS) * GROUP + j, 1)
                    row = xs[:, at, :].rearrange("p i d -> p (i d)")
                    act.activation(row, row, ACT.Identity, bias=nmr[:, at], scale=rstd1[:, at]).then_inc(S["xs_ok"], 1)
            with act.Fori(CHUNKS + GROUPS, EDGE_LOOPS) as i:
                indices(i)
            half = 3 * BANK
            act.wait_ge(S["edge_done"], EDGE_TILES + UNROLL + 1)
            act.activation(agg_sb[:, 0:half], ps_agg[:, 0:half], ACT.Copy).then_inc(S["agg_copied"], 1)
            act.wait_ge(S["w_lo_ok"], 2 * CHUNKS)
            for g in peeled(act, GROUPS):
                act.wait_ge(S["u_ps"], g + 1)
                freed(act, "h2_ps", g)
                act.activation(hid1T[0:F1, :], ps_u, ACT.Relu, scale=1.0 / Z_SCALE).then_inc(S["h1_ok"], 1)
                act.wait_ge(S["h2_ps"], g + 1)
                freed(act, "h3_ps", g)
                act.activation(hid2T[0:F2, :], ps_h2[0:F2, :], ACT.Relu).then_inc(S["h2_ok"], 1)
            act.wait_ge(S["aggr2"], TILES)
            act.activation(std[:, :], mv[:, :, 1], ACT.Sqrt, bias=eps_t[:, 0:1]).then_inc(S["std2_ok"], 1)
            for g in peeled(act, GROUPS):
                group = bass.ds(g * GROUP, GROUP)
                copy_transposed(g, xn2T, ("xn2T_ps", "xn2T_sb", "gates_ps"))
                act.activation(x_tab[:, group, 0:D], xs[:, group, :], ACT.Copy, scale=X_SCALE).then_inc(S["x_hi"], 1)
            act.wait_ge(S["exp_in"], 1)
            act.activation(ex, dlt, ACT.Exp).then_inc(S["exp_ok"], 1)

            def gelu(t):
                act.wait_ge(S["hb_ok"], t + 1)
                freed(act, "hT_ps", t)
                act.activation(hid32, hb, ACT.Gelu).then_inc(S["gelu_ok"], 1)

            def high_half(t):
                act.wait_ge(S["hT_ps"], t + 1)
                act.activation(hT_hi, ps_hT, ACT.Copy, scale=H_SCALE).then_inc(S["hT_hi_ok"], 1)

            def weigh(t):
                act.wait_ge(S["y_a_ok"], t + 1)
                freed(act, "y_scattered", 16 * t)
                act.activation(y_b, y_a, ACT.Copy, scale=slot_gate[:, bass.ds(t, 1)]).then_inc(S["y_ok"], 1)

            act.wait_ge(S["x_stored"], 16 * GROUPS)
            gelu(0)
            for t in peeled(act, SLOT_TILES - 1):
                high_half(t)
                gelu(t + 1)
                weigh(t)
            high_half(SLOT_TILES - 1)
            weigh(SLOT_TILES - 1)

        @block.tensor
        def _(pe):
            pe.wait_ge(S["zeros"], 4)
            with pe.Fori(0, WARM_UP) as _i:
                pe.matmul(ps[:, 7 * BANK:], zero16[:, 0:P], zeros_wide(BANK), start=True, stop=True)
            pe.wait_ge(S["params_in"], 16 * 6)
            pe.wait_ge(S["consts"], 1)

            def transposes(g, rows, names):
                n_rows, n_ps, n_sb = names
                for j in range(GROUP):
                    pe.wait_ge(S[n_rows], GROUP * g + (j + 1))
                    freed(pe, n_sb, GROUP * g + (j + 1 - GROUP))
                    for c in range(2):
                        last = pe.transpose(ps_t[j][:, c * P:(c + 1) * P], rows[:, j, c * P:(c + 1) * P], ident[:, :])
                    last.then_inc(S[n_ps], 1)

            def z_product(g):
                freed(pe, "z_lo", g - 1)
                for j in range(GROUP):
                    pe.wait_ge(S["xnT_sb"], GROUP * g + (j + 1))
                    for c in range(2):
                        last = pe.matmul(ps_z[g % 2][:, j * F1:(j + 1) * F1], xnT[g % 2][:, j, c * P:(c + 1) * P],
                                         w1g[:, c, :], start=c == 0, stop=c == 1)
                last.then_inc(S["z_ps"], 1)

            transposes(0, xn, ("xn_ok", "xnT_ps", "xnT_sb"))
            for g in range(GROUPS - 1):
                transposes(g + 1, xn, ("xn_ok", "xnT_ps", "xnT_sb"))
                z_product(g)
            z_product(GROUPS - 1)

            banks = [(a, min(a + BANK, NODES)) for a in range(0, NODES, BANK)]
            pe.wait_ge(S["zeros"], 4)
            pe.wait_ge(S["z_lo"], GROUPS)
            for a, b in banks:
                last = pe.matmul(ps_agg[:, a:b], zero16[:, 0:P], zeros_wide(b - a), start=True, stop=False,
                                 skip_group_check=True)
            last.then_inc(S["edge_done"], UNROLL)
            with pe.Fori(0, EDGE_LOOPS) as i:
                for j in range(UNROLL):
                    pe.wait_ge(z_in[j], 16 * i + 16)
                    pe.wait_ge(S["hot_ok"], UNROLL * i + (j + 1))
                    for a, b in banks:
                        last = pe.matmul(ps_agg[:, a:b], z_rows[:, j, :], hot[:, j % HOT_RING, a:b],
                                         start=False, stop=False, skip_group_check=True)
                    last.then_inc(S["edge_done"], 1)
            for a, b in banks:
                last = pe.matmul(ps_agg[:, a:b], zero16[:, 0:P], zeros_wide(b - a), start=False, stop=True,
                                 skip_group_check=True)
            last.then_inc(S["edge_done"], 1)

            pe.wait_ge(S["wident_ok"], 1)
            pe.wait_ge(S["agg_copied"], 3)
            def fold_halves(g):
                freed(pe, "h1_ok", g)
                pe.wait_ge(S["z_now_ok"], g + 1)
                for j in range(GROUP):
                    pe.matmul(ps_u[:, j * P:(j + 1) * P], fold[:, :], agg_sb[:, bass.ds(g * GROUP * P + j * P, P)],
                              start=True, stop=False)
                    last = pe.matmul(ps_u[:, j * P:(j + 1) * P], z_now[:, j, :], w_ident[:, :], start=False, stop=True)
                last.then_inc(S["u_ps"], 1)

            def middle(g):
                pe.wait_ge(S["h1_ok"], g + 1)
                freed(pe, "h2_ok", g)
                pe.matmul(ps_h2[:, 0:BANK], w2g[:, :], hid1T[0:F1, 0:BANK], start=True, stop=True)
                pe.matmul(ps_h2[:, BANK:], w2g[:, :], hid1T[0:F1, BANK:], start=True, stop=True).then_inc(S["h2_ps"], 1)

            def widen(g):
                pe.wait_ge(S["h2_ok"], g + 1)
                freed(pe, "x1_ok", g)
                for j in range(GROUP):
                    last = pe.matmul(ps_h3[:, j * D:(j + 1) * D], hid2T[0:F2, j * P:(j + 1) * P], w3g[:, :],
                                     start=True, stop=True)
                last.then_inc(S["h3_ps"], 1)

            fold_halves(0)
            for g in peeled(pe, GROUPS - 1):
                middle(g)
                fold_halves(g + 1)
                widen(g)
            middle(GROUPS - 1)
            widen(GROUPS - 1)

            pe.wait_ge(S["x1_ok"], GROUPS)

            def gates(g):
                for j in range(GROUP):
                    at = (g * GROUP + j) * EXPERTS
                    pe.wait_ge(S["xn2T_sb"], GROUP * g + (j + 1))
                    for c in range(2):
                        last = pe.matmul(ps_gate[:, at:at + EXPERTS], xn2T[:, j, c * P:(c + 1) * P], wgate[:, c, :],
                                         start=c == 0, stop=c == 1)
                last.then_inc(S["gates_ps"], 1)

            for g in range(GROUPS + 1):
                if g < GROUPS:
                    transposes(g, xs[:, g * GROUP:(g + 1) * GROUP, :], ("xn2_ok", "xn2T_ps", "xn2T_sb"))
                if g > 0:
                    gates(g - 1)

            pe.wait_ge(S["counts_in"], 1)
            pe.wait_ge(S["const2"], 4)
            pe.matmul(ps_count[:, 0:TE], before, tmp, start=True, stop=True)
            pe.matmul(ps_count[:, TE:], ones, tmp, start=True, stop=True).then_inc(S["counts_ps"], 1)
            pe.matmul(ps_slot, zero16[:, 0:P], zeros_wide(2 * SLOT_TILES), start=True, stop=False,
                      skip_group_check=True).then_inc(S["pair_done"], 2)
            with pe.Fori(0, TOPK * TILES // (2 * SLOT_COLS)) as i:
                for s in range(2):
                    pe.wait_ge(S["lo_hot_ok"], 2 * i + (s + 1))
                    pe.wait_ge(S["values_ok"], 4 * i + 2 * (s + 1))
                    for c in range(SLOT_COLS):
                        last = pe.matmul(ps_slot, lo_hot[:, s, c, :], val_hi[:, s, c].rearrange("p v n -> p (v n)"),
                                         start=False, stop=False, skip_group_check=True)
                    last.then_inc(S["pair_done"], 1)
            pe.matmul(ps_slot, zero16[:, 0:P], zeros_wide(2 * SLOT_TILES), start=False, stop=True,
                      skip_group_check=True).then_inc(S["slots_ps"], 1)

            def transpose_tokens(t):
                pe.wait_ge(S["tok_gathered"], 16 * t + 16)
                freed(pe, "tok_sb", t)
                for c in range(4):
                    last = pe.transpose(ps_xT[:, c * P:(c + 1) * P], x_rows[:, c * P:(c + 1) * P], ident16[:, :])
                last.then_inc(S["tok_ps"], 1)

            def first_product(t):
                ex_t = pe.value_load(tile_expert[0:1, bass.ds(t, 1)], min_val=0, max_val=EXPERTS - 1)
                pe.wait_ge(S["tok_sb"], t + 1)
                freed(pe, "hb_ok", t)
                for half in range(2):
                    o = ps_hid[:, half * BANK:(half + 1) * BANK]
                    for c in range(2):
                        at = bass.ds(ex_t * 2048 + (c * HID + half * BANK), BANK)
                        pe.matmul(o, xT[:, c * P:(c + 1) * P], w_hi[:, at], start=c == 0, stop=False)
                        pe.matmul(o, xT[:, (2 + c) * P:(3 + c) * P], w_hi[:, at], start=False, stop=False)
                        last = pe.matmul(o, xT[:, c * P:(c + 1) * P], w_lo[:, at], start=False, stop=c == 1)
                last.then_inc(S["hid_ps"], 1)

            def transpose_hidden(t):
                pe.wait_ge(S["gelu_ok"], t + 1)
                freed(pe, "hT_lo_ok", t)
                for m in range(HID // P):
                    last = pe.transpose(ps_hT[:, m * P:(m + 1) * P], hid32[:, m * P:(m + 1) * P], ident[:, :])
                last.then_inc(S["hT_ps"], 1)

            def second_product(t):
                ex_t = pe.value_load(tile_expert[0:1, bass.ds(t, 1)], min_val=0, max_val=EXPERTS - 1)
                pe.wait_ge(S["hT_lo_ok"], t + 1)
                freed(pe, "y_a_ok", t)
                n = HID // P
                for m in range(n):
                    at = bass.ds(ex_t * 2048 + (CHUNKS // 2 * 1024 + m * D), D)
                    pe.matmul(ps_y, hT_hi[:, m * P:(m + 1) * P], w_hi[:, at], start=m == 0, stop=False)
                    pe.matmul(ps_y, hT_lo[:, m * P:(m + 1) * P], w_hi[:, at], start=False, stop=False)
                    last = pe.matmul(ps_y, hT_hi[:, m * P:(m + 1) * P], w_lo[:, at], start=False, stop=m == n - 1)
                last.then_inc(S["y_ps"], 1)

            pe.wait_ge(S["tables_ok"], 1)
            pe.wait_ge(S["w_lo_ok"], 2 * CHUNKS)
            transpose_tokens(0)
            first_product(0)
            transpose_tokens(1)
            for t in peeled(pe, SLOT_TILES - 2):
                transpose_hidden(t)
                first_product(t + 1)
                transpose_tokens(t + 2)
                second_product(t)
            transpose_hidden(SLOT_TILES - 2)
            first_product(SLOT_TILES - 1)
            second_product(SLOT_TILES - 2)
            transpose_hidden(SLOT_TILES - 1)
            second_product(SLOT_TILES - 1)


def kernel(**inputs):
    import numpy as np
    import concourse.bacc as bacc
    from concourse.bass_utils import run_bass_kernel_spmd

    def grab(name):
        return np.ascontiguousarray(np.asarray(inputs[name]))

    def edges(name, fill):
        a = np.full((P * EDGE_TILES,), fill, np.int32)
        a[:EDGES] = grab(name)
        return a.reshape(P, EDGE_TILES)

    arrays = {
        "x": grab("x"),
        "src": edges("src", -1),
        "dst": edges("dst", 0),
        "w": grab("L0_gnn_w"),
        "w1gT": np.ascontiguousarray(grab("L0_gnn_W1").T),
        "w2gT": np.ascontiguousarray(grab("L0_gnn_W2").T),
        "w3gT": np.ascontiguousarray(grab("L0_gnn_W3").T),
        "wg": grab("L0_ffn_Wg"),
        "bg": grab("L0_ffn_bg"),
        "weights": np.concatenate([
            grab("L0_ffn_W1").reshape(-1, 1024),
            grab("L0_ffn_W2").reshape(EXPERTS, 2, 4, P, D).transpose(0, 1, 3, 2, 4).reshape(-1, 1024)]),
        "b1": grab("L0_ffn_b1").reshape(-1),
        "b2": grab("L0_ffn_b2").reshape(-1),
    }
    nc = bacc.Bacc("TRN2", target_bir_lowering=False, num_devices=1)
    args = [nc.dram_tensor(f"in_{n}", a.shape, mybir.dt.from_np(a.dtype), kind="ExternalInput").ap()
            for n, a in arrays.items()]
    out = nc.dram_tensor("out_0", (NODES, D), mybir.dt.float32, kind="ExternalOutput").ap()
    gnn_moe(nc, *args, out)
    r = run_bass_kernel_spmd(nc, [{f"in_{n}": a for n, a in arrays.items()}], core_ids=[0])
    return r.results[0]["out_0"]
```

```python
from contextlib import ExitStack

import concourse.bass as bass
from concourse import mybir

P = 128
NODES, D, EDGES = 3125, 256, 50000
F1, F2 = 64, 32
EXPERTS, HID, TOPK = 8, 1024, 2
TILES = -(-NODES // P)
ROWS = TILES * P
TAIL = NODES - (TILES - 1) * P
GROUP = 5
GROUPS = TILES // GROUP
UNROLL = 8
EDGE_TILES = -(-EDGES // (P * UNROLL)) * UNROLL
EDGE_LOOPS = EDGE_TILES // UNROLL
HOT_RING = 4
HOT_WORDS = (NODES + 1) // 2 + 1
BANK = 512
SLOT_TILES = (TOPK * NODES + EXPERTS * (P - 1)) // P
CHUNK = 1024
CHUNKS = 2 * EXPERTS * D * HID // (P * CHUNK)
HALF = CHUNK // 2
CENTER = NODES // 2
EPS = 1e-5
Z_SCALE, X_SCALE, W_SCALE, H_SCALE = 2.0**5, 2.0**11, 2.0**8, 2.0**4
PADDED_POSITION = 65536.0


def gnn_moe(nc, x, src, dst, w, w1gT, w2gT, w3gT, wg, bg, weights, b1, b2, out):
    fp32, fp16, i32 = mybir.dt.float32, mybir.dt.float16, mybir.dt.int32
    ALU, ACT, AX = mybir.AluOpType, mybir.ActivationFunctionType, mybir.AxisListType

    z_table = nc.dram_tensor("z_table", (ROWS, P), fp16).ap()
    x_table = nc.dram_tensor("x_table", (ROWS + P, 2 * D), fp16).ap()
    total = nc.dram_tensor("total", (ROWS + P, D), fp32).ap()

    ctx = ExitStack()
    with ctx:
        def sb(name, shape, dt=fp32):
            return ctx.enter_context(nc.sbuf_tensor(name, shape, dt))

        def sem(name):
            return ctx.enter_context(nc.semaphore(name))

        w_hi = sb("w_hi", [P, CHUNKS * CHUNK], fp16)
        w_lo = sb("w_lo", [P, CHUNKS * CHUNK], fp16)
        shared = sb("shared", [P, EXPERTS * HID])
        hot = shared[:, 0:HOT_RING * HOT_WORDS].bitcast(fp16).rearrange("p (r n) -> p r n", r=HOT_RING)
        node_iota = shared[:, HOT_RING * HOT_WORDS:(HOT_RING + 1) * HOT_WORDS].bitcast(fp16)[:, 0:NODES]
        agg_sb = shared[:, 0:ROWS]
        b1_rep = shared[:, :]
        xs = sb("xs", [P, TILES, D])
        z32 = sb("z32", [P, TILES, F1])
        stage = sb("stage", [P, 2, HALF])
        z_rows = sb("z_rows", [P, UNROLL, P], fp16)
        src_i = sb("src_i", [P, EDGE_TILES], i32)
        dst_i = sb("dst_i", [P, EDGE_TILES], i32)
        src_f = src_i[:, :].bitcast(fp32)
        dst_slot = sb("dst_slot", [P, UNROLL], i32)
        spare = w_lo[:, (CHUNKS - 16) * CHUNK:].bitcast(fp32)
        xn = spare[:, 0:GROUP * D].rearrange("p (j d) -> p j d", j=GROUP)
        xnT = [spare[:, n * GROUP * D:(n + 1) * GROUP * D].rearrange("p (j d) -> p j d", j=GROUP) for n in (1, 2)]
        z_tab = spare[:, 3 * GROUP * D:3 * GROUP * D + TILES * F1].bitcast(fp16).rearrange(
            "p (i c) -> p i c", i=TILES)
        hid1T = shared[:, ROWS:ROWS + GROUP * P]
        x_tab = shared[:, 0:TILES * D].bitcast(fp16).rearrange("p (i c) -> p i c", i=TILES)
        xn2T = [a.rearrange("p (j d) -> p j d", j=GROUP)
                for a in (shared[:, TILES * D:(TILES + GROUP) * D],
                          z32[:, :, :].rearrange("p i f -> p (i f)")[:, 0:GROUP * D])]
        hid2T = stage[:, :, :].rearrange("p s n -> p (s n)")[:, 0:GROUP * P // 2].bitcast(fp16)
        h3_sb = [shared[:, ROWS + GROUP * P + n * GROUP * D:ROWS + GROUP * P + (n + 1) * GROUP * D] for n in range(2)]
        z_now = stage[:, :, :].rearrange("p s n -> p (s n)")[:, GROUP * P:GROUP * P + GROUP * F1].rearrange(
            "p (j f) -> p j f", j=GROUP)
        w1g = sb("w1g", [P, 2, F1])
        w2g = sb("w2g", [F1, P])
        w3g = sb("w3g", [3 * F2, D])
        w3_parts = sb("w3_parts", [3 * F2, D], fp16)
        wgate = sb("wgate", [P, 2, EXPERTS])
        bg_rep = sb("bg_rep", [P, EXPERTS])
        w_rep = sb("w_rep", [P, 1])
        ident = sb("ident", [P, P])
        ident16 = sb("ident16", [P, P], fp16)
        w_ident = sb("w_ident", [P, P])
        fold = sb("fold", [P, F1])
        zero16 = sb("zero16", [P, P], fp16)
        eps_t = sb("eps_t", [P, 1])
        unread = sb("unread", [P, 1])
        bn = sb("bn", [P, TILES, 6])
        mv = sb("mv", [P, TILES, 2])
        std = sb("std", [P, TILES])
        rstd = sb("rstd", [P, TILES])
        nmr = sb("nmr", [P, TILES])
        rstd1 = sb("rstd1", [P, TILES])
        xs_flat = xs[:, :, :].rearrange("p i d -> p (i d)")
        TE = TILES * EXPERTS
        used = [0]

        def part(n):
            a = used[0]
            used[0] += n
            return xs_flat[:, a:a + n]

        def te(ap):
            return ap.rearrange("p (i e) -> p i e", e=EXPERTS)

        logits, eq, cand, first1, first2, logits2, both, tmp = (part(TE) for _ in range(8))
        total_em, scan_em, pos_all, tmp2 = (part(TE) for _ in range(4))
        ones_te = part(TE)
        v1, i1, v2, i2, dlt, ex, s1 = (part(TILES) for _ in range(7))
        gate2 = part(TOPK * TILES)
        pos2 = part(TOPK * TILES)
        pos_i = part(TOPK * TILES).bitcast(i32)
        hi_i = part(TOPK * TILES).bitcast(i32)
        lo_i = part(TOPK * TILES).bitcast(i32)
        hi_f, lo_f = part(TOPK * TILES), part(TOPK * TILES)
        tot_e, n_tiles, c_tiles, off_e, off2_e = (part(EXPERTS) for _ in range(5))
        n_int, n_int2 = part(EXPERTS).bitcast(i32), part(EXPERTS).bitcast(i32)
        tile_ge = stage[:, 1, 0:SLOT_TILES * EXPERTS]
        tile_e = part(SLOT_TILES)
        z_flat = z32[:, :, :].rearrange("p i f -> p (i f)")
        SLOT_COLS = 5
        lo_hot, hot_hi, val_hi = (part(2 * SLOT_COLS * n) for n in (P, SLOT_TILES, 2 * SLOT_TILES))
        lo_hot = lo_hot.rearrange("p (s c n) -> p s c n", s=2, c=SLOT_COLS)
        hot_hi = hot_hi.rearrange("p (s c n) -> p s c n", s=2, c=SLOT_COLS)
        val_hi = val_hi.rearrange("p (s c v n) -> p s c v n", s=2, c=SLOT_COLS, v=2)
        slot_row1, is_pad, pad_f = (z_flat[:, CHUNK + n * SLOT_TILES:CHUNK + (n + 1) * SLOT_TILES] for n in range(3))
        e_iota = sb("e_iota", [P, EXPERTS])
        valid = sb("valid", [P, TILES])
        pad_pos = sb("pad_pos", [P, TILES])
        rows_flat = z_rows[:, :, :].rearrange("p j c -> p (j c)").bitcast(fp32)
        lo_iota = rows_flat[:, 0:P]
        hi_iota = sb("hi_iota", [P, SLOT_TILES])
        row_iota = sb("row_iota", [P, TOPK * TILES])
        trash_iota = sb("trash_iota", [P, 1])
        before = rows_flat[:, P:2 * P]
        ones = rows_flat[:, 2 * P:3 * P]
        slot_row = sb("slot_row", [P, SLOT_TILES], i32)
        slot_gate = sb("slot_gate", [P, SLOT_TILES])
        tile_expert = sb("tile_expert", [P, SLOT_TILES], i32)
        tile_base = sb("tile_base", [P, SLOT_TILES], i32)
        tok_slot = sb("tok_slot", [P, 1], i32)
        dest_slot = sb("dest_slot", [P, 1], i32)
        b2_rep = xs_flat[:, TILES * D - EXPERTS * D:]
        hb = xs_flat[:, TILES * D - EXPERTS * D - HID:TILES * D - EXPERTS * D]
        assert used[0] <= TILES * D, used
        hid32 = stage[:, :, :].rearrange("p s n -> p (s n)")
        y_a = rows_flat[:, 0:D]
        y_b = rows_flat[:, D:2 * D]
        x_rows = z_flat[:, 0:D].bitcast(fp16)
        xT = z_flat[:, D:2 * D].bitcast(fp16)
        hT_hi = xs_flat[:, 0:HID // 2].bitcast(fp16)
        hT_lo = xs_flat[:, HID // 2:HID].bitcast(fp16)
        ps = ctx.enter_context(nc.psum_tensor("ps", [P, 8 * BANK], fp32))
        ps_t = [ps[:, j * BANK:j * BANK + D] for j in range(GROUP)]
        ps_z = [ps[:, b * BANK:b * BANK + GROUP * F1] for b in (5, 6)]
        ps_agg = ps[:, 0:NODES]
        ps_idle = ps[:, 6 * BANK:7 * BANK]
        ps_u = ps[0:F1, 0:GROUP * P]
        ps_h2 = ps[:, 2 * BANK:2 * BANK + GROUP * P]
        ps_h3 = ps[:, 4 * BANK:4 * BANK + GROUP * D]
        ps_gate = ps[:, 7 * BANK:7 * BANK + TE]
        ps_count = ps[:, 0:2 * TE]
        ps_slot = ps[:, BANK:BANK + 2 * SLOT_TILES]
        ps_hid = ps[:, 0:HID]
        ps_hT = ps[:, 2 * BANK:2 * BANK + HID]
        ps_xT = ps[:, 4 * BANK:4 * BANK + D].bitcast(fp16)
        ps_y = ps[:, 5 * BANK:5 * BANK + D]

        S = {n: sem(n) for n in (
            "table_loaded params_in edges_in consts const2 zeros const_chain zero_rows w3_hi_ok w3_ok "
            "stats aggr std_ok rstd_ok rstd1_ok nmr_ok xn_ok z_now_ok h2_hi h3_sb_ok "
            "xs_ok xnT_ps xnT_sb z_ps z32_ok z_hi z_lo z_stored src_ok wident_ok idx_copied "
            "hot_ok edge_done w_hi_ok w_lo_ok agg_copied u_ps h1_ok h2_ps h2_ok h3_ps x1_ok "
            "stats2 aggr2 std2_ok rstd2_ok nmr2_ok xn2_ok xn2T_ps xn2T_sb gates_ps x_hi x_lo "
            "x_stored chain exp_in exp_ok counts_in counts_ps lo_hot_ok values_ok hot_hi_ok pair_done slots_ps "
            "tables_ok biases_in biases2_in tok_gathered tok_ps tok_sb hid_ps hb_ok gelu_ok hT_ps hT_hi_ok "
            "hT_lo_ok y_ps y_a_ok y_ok y_scattered tok_idx dest_idx out_stored"
        ).split()}
        held = {e.engine: sem(f"held{n}") for n, e in enumerate((nc.gpsimd, nc.vector))}
        z_in = [sem(f"z_in{j}") for j in range(UNROLL)]
        w_in = [sem(f"w_in{s}") for s in range(2)]
        x_in = [sem(f"x_in{g}") for g in range(GROUPS)]
        x1_stored = [sem(f"x1_stored{g}") for g in range(GROUPS)]

        table_z = z_table.rearrange("(i p) c -> p i c", p=P)
        table_x = x_table.rearrange("(i p) c -> p i c", p=P)
        table_x1 = total.rearrange("(i p) c -> p i c", p=P)
        wflat = weights.rearrange("(q p) n -> q p n", p=P)
        full = TILES - 1
        BATCHES_1 = (slice(0, 3 * GROUP), slice(3 * GROUP, TILES))
        BATCHES_2 = (slice(0, 3 * GROUP), slice(3 * GROUP, TILES))
        PARAMS = 10

        def zeros_wide(n):
            return zero16[:, 0:1].broadcast_to([P, n])

        def bcast(ap, n):
            return ap.rearrange("p (o k) -> p o k", o=1).broadcast_to([P, n, ap.shape[1]])

        def bcast_in(ap, n):
            return ap.rearrange("p (k o) -> p k o", o=1).broadcast_to([P, ap.shape[1], n])

        def peeled(eng, n):
            yield 0
            with eng.Fori(1, n) as i:
                yield i

        def freed(eng, name, n):
            if not (isinstance(n, int) and n <= 0):
                eng.wait_ge(S[name], n)

        def hold(eng):
            eng.sem_inc(held[eng.engine], 1)

        block = ctx.enter_context(nc.Block())

        @block.sync
        def _(sp):
            for g in range(GROUPS):
                tiles = slice(g * GROUP, min((g + 1) * GROUP, full))
                sp.dma_start(xs[:, tiles, :], x[tiles.start * P:tiles.stop * P, :].rearrange(
                    "(i p) d -> p i d", p=P)).then_inc(x_in[g], 16)
            sp.wait_ge(S["zeros"], 1)
            sp.dma_start(xs[0:TAIL, full, :], x[full * P:NODES, :]).then_inc(x_in[GROUPS - 1], 16)
            sp.dma_start(w1g[:, :, :], w1gT.rearrange("(c p) f -> p c f", p=P)).then_inc(S["params_in"], 16)
            for n in range(3):
                sp.dma_start(w2g[:, n * F2:(n + 1) * F2], w2gT).then_inc(S["params_in"], 16)
                sp.dma_start(w3g[n * F2:(n + 1) * F2, :], w3gT).then_inc(S["params_in"], 16)
            sp.dma_start(wgate[:, :, :], wg.rearrange("(c p) e -> p c e", p=P)).then_inc(S["params_in"], 16)
            sp.dma_start(bg_rep[:, :], bg.rearrange("(o e) -> o e", o=1).broadcast_to([P, EXPERTS])).then_inc(S["params_in"], 16)
            sp.dma_start(w_rep[:, :], w.rearrange("(o e) -> o e", o=1).broadcast_to([P, 1])).then_inc(S["params_in"], 16)
            sp.dma_start(src_i[:, :], src).then_inc(S["edges_in"], 16)
            sp.dma_start(dst_i[:, :], dst).then_inc(S["edges_in"], 16)
            with sp.Fori(0, GROUPS) as g:
                sp.wait_ge(S["z_lo"], g + 1)
                sp.dma_start(table_z[:, bass.ds(g * GROUP, GROUP), :],
                             z_tab[:, bass.ds(g * GROUP, GROUP), :]).then_inc(S["z_stored"], 16)
            for s in range(2):
                sp.dma_start(stage[:, s, :], wflat[0, :, s * HALF:(s + 1) * HALF]).then_inc(w_in[s], 16)
            with sp.Fori(1, CHUNKS) as i:
                for s in range(2):
                    sp.wait_ge(S["w_lo_ok"], 2 * i + (s - 1))
                    sp.dma_start(stage[:, s, :], wflat[bass.ds(i, 1), :, s * HALF:(s + 1) * HALF].rearrange(
                        "q p n -> p (q n)")).then_inc(w_in[s], 16)
            sp.wait_ge(S["zeros"], 4)
            zeros32 = zero16[:, :].bitcast(fp32)
            for table, n in ((x_table.bitcast(fp32), D), (total, D)):
                sp.dma_start(table[ROWS:, :].rearrange("p (a b) -> p a b", b=P // 2),
                             zeros32.rearrange("p (o b) -> p o b", o=1).broadcast_to([P, n * 2 // P, P // 2])
                             ).then_inc(S["zero_rows"], 16)
            for g in range(GROUPS):
                group = slice(g * GROUP, (g + 1) * GROUP)
                sp.wait_ge(S["x1_ok"], g + 1)
                sp.dma_start(table_x1[:, group, :], xs[:, group, :]).then_inc(x1_stored[g], 16)
            with sp.Fori(0, GROUPS) as g:
                sp.wait_ge(S["x_lo"], g + 1)
                sp.dma_start(table_x[:, bass.ds(g * GROUP, GROUP), :],
                             x_tab[:, bass.ds(g * GROUP, GROUP), :]).then_inc(S["x_stored"], 16)
            sp.wait_ge(S["gates_ps"], GROUPS)
            sp.wait_ge(S["x_stored"], 16 * GROUPS)
            sp.dma_start(b1_rep, b1.rearrange("(o n) -> o n", o=1).broadcast_to([P, EXPERTS * HID])).then_inc(S["biases_in"], 16)
            sp.wait_ge(S["slots_ps"], 1)
            sp.dma_start(b2_rep, b2.rearrange("(o n) -> o n", o=1).broadcast_to([P, EXPERTS * D])).then_inc(S["biases2_in"], 16)
            sp.wait_ge(S["y_scattered"], 16 * SLOT_TILES)
            sp.dma_start(out.rearrange("n d -> (n d)").rearrange("(k m) -> k m", k=P),
                         total[0:NODES, :].rearrange("n d -> (n d)").rearrange("(k m) -> k m", k=P)
                         ).then_inc(S["out_stored"], 16)
            sp.wait_ge(S["out_stored"], 16)

        @block.gpsimd
        def _(pool):
            pool.memset(ident[:, :], 0.0).then_inc(S["const_chain"], 1)
            pool.memset(ident16[:, :], 0.0).then_inc(S["const_chain"], 1)
            pool.memset(fold[:, :], 0.0).then_inc(S["const_chain"], 1)
            pool.memset(valid[:, :], 1.0).then_inc(S["const_chain"], 1)
            pool.memset(pad_pos[:, :], 0.0).then_inc(S["const_chain"], 1)
            pool.wait_ge(S["const_chain"], 5)

            def select(ap, op, fill, base, pattern, mult):
                pool.affine_select(out=ap, in_=ap, compare_op=op, fill=fill, base=base,
                                   pattern=pattern, channel_multiplier=mult).then_inc(S["const_chain"], 1)

            select(ident[:, :], ALU.not_equal, 1.0, 0, [[-1, P]], 1)
            select(ident16[:, :], ALU.not_equal, 1.0, 0, [[-1, P]], 1)
            select(fold[:, :], ALU.not_equal, 1.0, 0, [[-1, F1]], 1)
            select(valid[:, full:TILES], ALU.is_gt, 0.0, TAIL, [[0, 1]], -1)
            select(pad_pos[:, full:TILES], ALU.is_gt, PADDED_POSITION, TAIL, [[0, 1]], -1)
            pool.wait_ge(S["const_chain"], 10)
            select(fold[:, :], ALU.not_equal, 1.0, -F1, [[-1, F1]], 1)
            imprecise = dict(allow_small_or_imprecise_dtypes=True)
            for ap, pattern, base, mult in (
                (node_iota, [[1, NODES]], -CENTER, 0),
                (e_iota[:, :], [[1, EXPERTS]], -EXPERTS, 0),
                (hi_iota[:, :], [[1, SLOT_TILES]], 0, 0),
                (row_iota[:, :], [[0, TOPK], [P, TILES]], 1, 1),
                (trash_iota[:, :], [[0, 1]], ROWS + 1, 1),
            ):
                pool.iota(ap, pattern=pattern, base=base, channel_multiplier=mult, **imprecise).then_inc(S["const_chain"], 1)
            pool.wait_ge(S["const_chain"], 16)
            pool.memset(dest_slot[:, :], 0).then_inc(S["consts"], 1)

            pool.wait_ge(S["edges_in"], 32)
            pool.wait_ge(S["z_stored"], 16 * GROUPS)
            with pool.Fori(0, EDGE_LOOPS) as i:
                for j in range(UNROLL):
                    pool.wait_ge(S["idx_copied"], UNROLL * i + (j + 1))
                    hold(pool)
                    pool.indirect_dma_start(
                        out=z_rows[:, j, :], out_offset=None, in_=z_table,
                        in_offset=bass.IndirectOffsetOnAxis(ap=dst_slot[:, j:j + 1], axis=0)).then_inc(z_in[j], 16)

            pool.wait_ge(S["w_lo_ok"], 2 * CHUNKS)
            for g in peeled(pool, GROUPS):
                freed(pool, "u_ps", g)
                pool.tensor_copy(z_now[:, :, :], z32[:, bass.ds(g * GROUP, GROUP), :]).then_inc(S["z_now_ok"], 1)
            pool.wait_ge(S["edge_done"], EDGE_TILES + UNROLL + 1)
            pool.memset(ones, 1.0).then_inc(S["const2"], 1)
            pool.memset(before, 1.0).then_inc(S["const2"], 1)
            pool.iota(lo_iota, pattern=[[1, P]], base=0, channel_multiplier=0, **imprecise).then_inc(S["const2"], 1)
            pool.wait_ge(S["const2"], 2)
            pool.affine_select(out=before, in_=before, compare_op=ALU.is_gt, fill=0.0, base=0,
                               pattern=[[1, P]], channel_multiplier=-1).then_inc(S["const2"], 1)

            pool.sem_inc(S["values_ok"], 4)
            with pool.Fori(0, TOPK * TILES // (2 * SLOT_COLS)) as i:
                for s in range(2):
                    cols = bass.ds(i * (2 * SLOT_COLS) + s * SLOT_COLS, SLOT_COLS)
                    pool.wait_ge(S["pair_done"], 2 * i + (s + 1))
                    pool.wait_ge(S["hot_hi_ok"], 2 * i + (s + 1))
                    for v, values in enumerate((row_iota, gate2)):
                        pool.tensor_tensor(val_hi[:, s, :, v, :], hot_hi[:, s], bcast_in(values[:, cols], SLOT_TILES),
                                           ALU.mult).then_inc(S["values_ok"], 1)

            pool.wait_ge(S["tables_ok"], 1)
            pool.wait_ge(S["x_stored"], 16 * GROUPS)
            pool.wait_ge(S["zero_rows"], 32)

            def gather(t):
                pool.tensor_copy(tok_slot[:, :], slot_row[:, bass.ds(t, 1)]).then_inc(S["tok_idx"], 1)
                pool.wait_ge(S["tok_idx"], t + 1)
                hold(pool)
                pool.indirect_dma_start(
                    out=x_rows, out_offset=None, in_=x_table,
                    in_offset=bass.IndirectOffsetOnAxis(ap=tok_slot[:, 0:1], axis=0)).then_inc(S["tok_gathered"], 16)

            def scatter(t):
                freed(pool, "y_scattered", 16 * t)
                pool.tensor_copy(dest_slot[:, :], slot_row[:, bass.ds(t, 1)]).then_inc(S["dest_idx"], 1)
                pool.wait_ge(S["dest_idx"], t + 1)
                pool.wait_ge(S["y_ok"], t + 1)
                hold(pool)
                pool.indirect_dma_start(
                    out=total, out_offset=bass.IndirectOffsetOnAxis(ap=dest_slot[:, 0:1], axis=0),
                    in_=y_b, in_offset=None, compute_op=ALU.add).then_inc(S["y_scattered"], 16)

            gather(0)
            for t in (1, 2):
                pool.wait_ge(S["tok_ps"], t)
                gather(t)
            for t in peeled(pool, SLOT_TILES - 3):
                pool.wait_ge(S["tok_ps"], t + 3)
                gather(t + 3)
                scatter(t)
            for t in range(SLOT_TILES - 3, SLOT_TILES):
                scatter(t)

        @block.vector
        def _(dve):
            dve.memset(xs[:, full:TILES, :], 0.0).then_inc(S["zeros"], 1)
            dve.memset(eps_t[:, :], EPS).then_inc(S["zeros"], 1)
            dve.memset(w2g[:, 3 * F2:], 0.0).then_inc(S["zeros"], 1)
            dve.memset(zero16[:, :], 0.0).then_inc(S["zeros"], 1)

            def stats(g, names):
                n_stats, n_aggr = names
                for i in range(g * GROUP, (g + 1) * GROUP):
                    dve.bn_stats(bn[:, i, :], xs[:, i, :]).then_inc(S[n_stats], 1)
                dve.wait_ge(S[n_stats], (g + 1) * GROUP)
                for i in range(g * GROUP, (g + 1) * GROUP):
                    dve.bn_aggr(mv[:, i, :], bn[:, i, :]).then_inc(S[n_aggr], 1)

            def scales(batches, b, n_std, n_rstd, n_nmr):
                part = batches[b]
                dve.wait_ge(S[n_std], b + 1)
                dve.reciprocal(rstd[:, part], std[:, part]).then_inc(S[n_rstd], 1)
                dve.wait_ge(S[n_rstd], b + 1)
                dve.scalar_tensor_tensor(nmr[:, part], mv[:, part, 0], -1.0, rstd[:, part],
                                         ALU.mult, ALU.mult).then_inc(S[n_nmr], 1)
                dve.wait_ge(S[n_nmr], b + 1)

            def normalize(g):
                for j in range(GROUP):
                    i = bass.ds(g * GROUP + j, 1)
                    freed(dve, "xnT_ps", GROUP * g + (j + 1 - GROUP))
                    dve.tensor_scalar(xn[:, j, :], xs[:, i, :].rearrange("p i d -> p (i d)"),
                                      rstd[:, i], nmr[:, i], ALU.mult, ALU.add).then_inc(S["xn_ok"], 1)

            def x_stats(g):
                dve.wait_ge(x_in[g], 32 if g == GROUPS - 1 else 16)
                stats(g, ("stats", "aggr"))

            def z_halves(g):
                group = slice(g * GROUP, (g + 1) * GROUP)
                dve.wait_ge(S["z_ps"], g + 1)
                pz = ps_z[g % 2].rearrange("p (j f) -> p j f", f=F1)
                dve.tensor_scalar(z32[:, group, :], pz, Z_SCALE, None, ALU.mult).then_inc(S["z32_ok"], 1)
                dve.tensor_scalar(z_tab[:, group, 0:F1], pz, Z_SCALE, None, ALU.mult).then_inc(S["z_hi"], 1)
                dve.wait_ge(S["z32_ok"], g + 1)
                dve.wait_ge(S["z_hi"], g + 1)
                dve.tensor_tensor(z_tab[:, group, F1:P], z32[:, group, :], z_tab[:, group, 0:F1],
                                  ALU.subtract).then_inc(S["z_lo"], 1)

            for g in range(3):
                x_stats(g)
            scales(BATCHES_1, 0, "std_ok", "rstd_ok", "nmr_ok")
            normalize(0)
            normalize(1)
            x_stats(3)
            normalize(2)
            z_halves(0)
            x_stats(4)
            scales(BATCHES_1, 1, "std_ok", "rstd_ok", "nmr_ok")
            normalize(3)
            z_halves(1)
            normalize(4)
            for g in range(2, GROUPS):
                z_halves(g)
            dve.tensor_scalar(rstd1[:, :], rstd[:, :], 1.0, None, ALU.add).then_inc(S["rstd1_ok"], 1)
            dve.wait_ge(S["params_in"], 16 * PARAMS)
            dve.wait_ge(S["consts"], 1)
            dve.tensor_scalar(w_ident[:, :], ident[:, :], w_rep[:, 0:1], None, ALU.mult).then_inc(S["wident_ok"], 1)
            dve.tensor_scalar(w3_parts[:, :], w3g[:, :], W_SCALE, None, ALU.mult).then_inc(S["w3_hi_ok"], 1)
            dve.wait_ge(S["w3_hi_ok"], 1)
            low = slice(2 * F2, 3 * F2)
            dve.scalar_tensor_tensor(w3_parts[low, :], w3g[low, :], W_SCALE, w3_parts[low, :],
                                     ALU.mult, ALU.subtract).then_inc(S["w3_ok"], 1)
            dve.wait_ge(S["edges_in"], 32)
            dve.tensor_scalar(src_f, src_i[:, :], float(-CENTER), None, ALU.add).then_inc(S["src_ok"], 1)
            dve.wait_ge(S["src_ok"], 1)
            dve.wait_ge(S["z_stored"], 16 * GROUPS)

            def one_hots(i):
                for j in range(UNROLL):
                    dve.wait_ge(S["edge_done"], UNROLL * i + (j + 1 + UNROLL - HOT_RING))
                    dve.tensor_scalar(hot[:, j % HOT_RING, 0:NODES], node_iota,
                                      src_f[:, bass.ds(i * UNROLL + j, 1)], None,
                                      ALU.is_equal).then_inc(S["hot_ok"], 1)

            with dve.Fori(0, CHUNKS) as i:
                one_hots(i)
                for s in range(2):
                    dve.wait_ge(S["w_hi_ok"], 2 * i + (s + 1))
                    dve.scalar_tensor_tensor(w_lo[:, bass.ds(i * CHUNK + s * HALF, HALF)], stage[:, s, :], W_SCALE,
                                             w_hi[:, bass.ds(i * CHUNK + s * HALF, HALF)],
                                             ALU.mult, ALU.subtract).then_inc(S["w_lo_ok"], 1)
            with dve.Fori(CHUNKS, EDGE_LOOPS) as i:
                one_hots(i)

            half = 3 * BANK
            dve.wait_ge(S["edge_done"], EDGE_TILES + UNROLL + 1)
            dve.memset(agg_sb[:, NODES:ROWS], 0.0).then_inc(S["agg_copied"], 1)
            dve.tensor_copy(agg_sb[:, half:NODES], ps_agg[:, half:NODES]).then_inc(S["agg_copied"], 1)
            def low_h2(g):
                low = slice(F2, 2 * F2)
                dve.wait_ge(S["h2_hi"], g + 1)
                dve.scalar_tensor_tensor(hid2T[low, :], ps_h2[low, :], 0.0, hid2T[low, :],
                                         ALU.max, ALU.subtract).then_inc(S["h2_ok"], 1)

            def x1_rows(g):
                rows = xs[:, g * GROUP:(g + 1) * GROUP, :].rearrange("p j d -> p (j d)")
                dve.wait_ge(S["h3_sb_ok"], g + 1)
                dve.tensor_tensor(rows, h3_sb[g % 2], rows, ALU.add).then_inc(S["x1_ok"], 1)
                dve.wait_ge(S["x1_ok"], g + 1)
                stats(g, ("stats2", "aggr2"))

            def x_low(g):
                group = slice(g * GROUP, (g + 1) * GROUP)
                dve.wait_ge(S["x_hi"], g + 1)
                dve.scalar_tensor_tensor(x_tab[:, group, D:2 * D], xs[:, group, :], X_SCALE, x_tab[:, group, 0:D],
                                         ALU.mult, ALU.subtract).then_inc(S["x_lo"], 1)

            def normalize_x1(g):
                dve.wait_ge(x1_stored[g], 16)
                for i in range(g * GROUP, (g + 1) * GROUP):
                    dve.tensor_scalar(xs[:, i, :], xs[:, i, :], rstd[:, i:i + 1], nmr[:, i:i + 1],
                                      ALU.mult, ALU.add).then_inc(S["xn2_ok"], 1)

            dve.wait_ge(S["xs_ok"], TILES)
            low_h2(0)
            for g in range(GROUPS - 1):
                low_h2(g + 1)
                x1_rows(g)
            scales(BATCHES_2, 0, "std2_ok", "rstd2_ok", "nmr2_ok")
            normalize_x1(0)
            normalize_x1(1)
            x1_rows(GROUPS - 1)
            scales(BATCHES_2, 1, "std2_ok", "rstd2_ok", "nmr2_ok")
            for g in range(2, GROUPS):
                normalize_x1(g)
            for g in range(GROUPS):
                x_low(g)

            chain = [0]

            def step(ins):
                chain[0] += 1
                ins.then_inc(S["chain"], 1)
                dve.wait_ge(S["chain"], chain[0])

            dve.wait_ge(S["gates_ps"], GROUPS)
            dve.wait_ge(S["x_lo"], GROUPS)
            dve.wait_ge(S["const2"], 4)
            e_b = bcast(e_iota[:, :], TILES)
            step(dve.tensor_tensor(te(logits), te(ps_gate), bcast(bg_rep[:, :], TILES), ALU.add))

            def first_of(values, v, idx, mask):
                step(dve.tensor_reduce(v, te(values), AX.X, ALU.max))
                step(dve.tensor_tensor(te(eq), te(values), bcast_in(v, EXPERTS), ALU.is_equal))
                step(dve.scalar_tensor_tensor(te(cand), te(eq), -float(EXPERTS), e_b, ALU.mult, ALU.add))
                step(dve.tensor_reduce(idx, te(cand), AX.X, ALU.min))
                step(dve.tensor_tensor(te(mask), te(cand), bcast_in(idx, EXPERTS), ALU.is_equal))

            first_of(logits, v1, i1, first1)
            step(dve.scalar_tensor_tensor(logits2, first1, -3.0e38, logits, ALU.mult, ALU.add))
            first_of(logits2, v2, i2, first2)
            dve.tensor_tensor(dlt, v2, v1, ALU.subtract).then_inc(S["exp_in"], 1)
            step(dve.tensor_tensor(both, first1, first2, ALU.add))
            dve.tensor_tensor(te(tmp), te(both), bcast_in(valid[:, :], EXPERTS), ALU.mult).then_inc(S["counts_in"], 1)
            step(dve.memset(ones_te, 1.0))
            dve.wait_ge(S["exp_ok"], 1)
            step(dve.tensor_scalar(s1, ex, 1.0, None, ALU.add))
            step(dve.reciprocal(gate2[:, 0:TILES], s1))
            step(dve.tensor_tensor(gate2[:, TILES:], ex, gate2[:, 0:TILES], ALU.mult))
            dve.wait_ge(S["counts_ps"], 1)
            em = lambda ap: ap.rearrange("p (e i) -> p e i", e=EXPERTS)
            step(dve.tensor_copy(em(total_em), ps_count[:, TE:].rearrange("p (i e) -> p e i", e=EXPERTS)))
            step(dve.tensor_tensor_scan(scan_em, ones_te, total_em, 0.0, ALU.mult, ALU.add))
            step(dve.tensor_reduce(tot_e, em(total_em), AX.X, ALU.add))
            step(dve.tensor_tensor(scan_em, scan_em, total_em, ALU.subtract))
            step(dve.tensor_scalar(n_int, tot_e, float(P - 1), None, ALU.add))
            step(dve.tensor_scalar(n_int2, n_int, 7, None, ALU.logical_shift_right))
            step(dve.tensor_copy(n_tiles, n_int2))
            step(dve.tensor_tensor_scan(c_tiles, ones_te[:, 0:EXPERTS], n_tiles, 0.0, ALU.mult, ALU.add))
            step(dve.tensor_tensor(off_e, c_tiles, n_tiles, ALU.subtract))
            step(dve.scalar_tensor_tensor(off2_e, off_e, float(P), em(scan_em)[:, :, 0], ALU.mult, ALU.subtract))
            step(dve.tensor_tensor(te(pos_all), te(ps_count[:, 0:TE]), bcast(off2_e, TILES), ALU.add))
            step(dve.tensor_tensor(te(tmp2), te(pos_all), scan_em.rearrange("p (e i) -> p i e", e=EXPERTS), ALU.add))
            for k, mask in enumerate((first1, first2)):
                pk = pos2[:, k * TILES:(k + 1) * TILES]
                step(dve.tensor_tensor(eq, mask, tmp2, ALU.mult))
                step(dve.tensor_reduce(pk, te(eq), AX.X, ALU.add))
                step(dve.tensor_tensor(pk, pk, pad_pos[:, :], ALU.add))
            step(dve.tensor_copy(pos_i, pos2))
            step(dve.tensor_scalar(hi_i, pos_i, 7, None, ALU.logical_shift_right))
            step(dve.tensor_scalar(lo_i, pos_i, P - 1, None, ALU.bitwise_and))
            step(dve.tensor_copy(hi_f, hi_i))
            step(dve.tensor_copy(lo_f, lo_i))
            tge = tile_ge.rearrange("p (t e) -> p t e", e=EXPERTS)
            step(dve.tensor_tensor(tge, bcast_in(hi_iota[:, :], EXPERTS), bcast(c_tiles, SLOT_TILES), ALU.is_ge))
            step(dve.tensor_reduce(tile_e, tge, AX.X, ALU.add))
            step(dve.tensor_scalar(tile_expert[:, :], tile_e, float(EXPERTS - 1), None, ALU.min))
            step(dve.tensor_scalar(tile_base[:, :], tile_e, float(EXPERTS - 1), float(2 * HID), ALU.min, ALU.mult))
            with dve.Fori(0, TOPK * TILES // (2 * SLOT_COLS)) as i:
                for s in range(2):
                    cols = bass.ds(i * (2 * SLOT_COLS) + s * SLOT_COLS, SLOT_COLS)
                    dve.wait_ge(S["values_ok"], 4 * i + 2 * (s + 1))
                    dve.tensor_tensor(hot_hi[:, s], bcast(hi_iota[:, :], SLOT_COLS),
                                      bcast_in(hi_f[:, cols], SLOT_TILES), ALU.is_equal).then_inc(S["hot_hi_ok"], 1)
                    dve.wait_ge(S["pair_done"], 2 * i + (s + 1))
                    dve.tensor_tensor(lo_hot[:, s], bcast(lo_iota, SLOT_COLS), bcast_in(lo_f[:, cols], P),
                                      ALU.is_equal).then_inc(S["lo_hot_ok"], 1)
            dve.wait_ge(S["slots_ps"], 1)
            step(dve.tensor_copy(slot_row1, ps_slot[:, 0:SLOT_TILES]))
            step(dve.tensor_copy(slot_gate[:, :], ps_slot[:, SLOT_TILES:]))
            step(dve.tensor_scalar(is_pad, slot_row1, 0.5, None, ALU.is_lt))
            step(dve.tensor_scalar(pad_f, is_pad, trash_iota[:, 0:1], -1.0, ALU.mult, ALU.add))
            dve.tensor_tensor(slot_row[:, :], slot_row1, pad_f, ALU.add).then_inc(S["tables_ok"], 1)

            def copy_xT(t):
                dve.wait_ge(S["tok_ps"], t + 1)
                dve.tensor_copy(xT, ps_xT).then_inc(S["tok_sb"], 1)

            def add_b1(t):
                ex_t = dve.value_load(tile_expert[0:1, bass.ds(t, 1)], min_val=0, max_val=EXPERTS - 1)
                dve.wait_ge(S["hid_ps"], t + 1)
                dve.scalar_tensor_tensor(hb, ps_hid, 1.0 / (X_SCALE * W_SCALE), b1_rep[:, bass.ds(ex_t * HID, HID)],
                                         ALU.mult, ALU.add).then_inc(S["hb_ok"], 1)

            def low_half(t):
                dve.wait_ge(S["hT_hi_ok"], t + 1)
                dve.scalar_tensor_tensor(hT_lo, ps_hT, H_SCALE, hT_hi, ALU.mult, ALU.subtract).then_inc(S["hT_lo_ok"], 1)

            def add_b2(t):
                ex_t = dve.value_load(tile_expert[0:1, bass.ds(t, 1)], min_val=0, max_val=EXPERTS - 1)
                dve.wait_ge(S["y_ps"], t + 1)
                freed(dve, "y_ok", t)
                dve.scalar_tensor_tensor(y_a, ps_y, 1.0 / (H_SCALE * W_SCALE), b2_rep[:, bass.ds(ex_t * D, D)],
                                         ALU.mult, ALU.add).then_inc(S["y_a_ok"], 1)

            dve.wait_ge(S["tables_ok"], 1)
            dve.wait_ge(S["biases_in"], 16)
            copy_xT(0)
            add_b1(0)
            copy_xT(1)
            dve.wait_ge(S["biases2_in"], 16)
            for t in peeled(dve, SLOT_TILES - 2):
                low_half(t)
                add_b1(t + 1)
                copy_xT(t + 2)
                add_b2(t)
            low_half(SLOT_TILES - 2)
            add_b1(SLOT_TILES - 1)
            add_b2(SLOT_TILES - 2)
            low_half(SLOT_TILES - 1)
            add_b2(SLOT_TILES - 1)

        @block.scalar
        def _(act):
            act.wait_ge(S["zeros"], 4)

            def load_table(function):
                act.activation(unread[:, :], eps_t[:, :], function).then_inc(S["table_loaded"], 1)

            def deviations(part, n_aggr, n_std):
                act.wait_ge(S[n_aggr], part.stop)
                act.activation(std[:, part], mv[:, part, 1], ACT.Sqrt, bias=eps_t[:, 0:1]).then_inc(S[n_std], 1)

            load_table(ACT.Sqrt)
            deviations(BATCHES_1[0], "aggr", "std_ok")

            def copy_transposed(g, target, names, buffers=1):
                n_ps, n_sb, n_free = names
                freed(act, n_free, g + 1 - buffers)
                for j in range(GROUP):
                    act.wait_ge(S[n_ps], GROUP * g + (j + 1))
                    act.activation(target[:, j, :], ps_t[j], ACT.Copy).then_inc(S[n_sb], 1)

            for g in range(GROUPS):
                copy_transposed(g, xnT[g % 2], ("xnT_ps", "xnT_sb", "z_ps"), 2)
                if g == 2:
                    deviations(BATCHES_1[1], "aggr", "std_ok")
            act.wait_ge(S["z_stored"], 16 * GROUPS)

            def indices(i):
                for j in range(UNROLL):
                    act.wait_ge(S["edge_done"], UNROLL * i + (j + 1))
                    act.activation(dst_slot[:, j:j + 1], dst_i[:, bass.ds(i * UNROLL + j, 1)],
                                   ACT.Copy).then_inc(S["idx_copied"], 1)

            act.wait_ge(S["edges_in"], 32)
            act.wait_ge(S["rstd1_ok"], 1)
            with act.Fori(0, CHUNKS) as i:
                indices(i)
                for s in range(2):
                    act.wait_ge(w_in[s], 16 * i + 16)
                    act.activation(w_hi[:, bass.ds(i * CHUNK + s * HALF, HALF)], stage[:, s, :], ACT.Copy,
                                   scale=W_SCALE).then_inc(S["w_hi_ok"], 1)
            with act.Fori(CHUNKS, CHUNKS + GROUPS) as i:
                indices(i)
                for j in range(GROUP):
                    at = bass.ds((i - CHUNKS) * GROUP + j, 1)
                    row = xs[:, at, :].rearrange("p i d -> p (i d)")
                    act.activation(row, row, ACT.Identity, bias=nmr[:, at], scale=rstd1[:, at]).then_inc(S["xs_ok"], 1)
            with act.Fori(CHUNKS + GROUPS, EDGE_LOOPS) as i:
                indices(i)
            half = 3 * BANK
            act.wait_ge(S["edge_done"], EDGE_TILES + UNROLL + 1)
            act.activation(agg_sb[:, 0:half], ps_agg[:, 0:half], ACT.Copy).then_inc(S["agg_copied"], 1)
            act.wait_ge(S["w_lo_ok"], 2 * CHUNKS)

            def h3_rows(g):
                act.wait_ge(S["h3_ps"], g + 1)
                freed(act, "x1_ok", g - 1)
                act.activation(h3_sb[g % 2], ps_h3, ACT.Relu, scale=1.0 / (H_SCALE * W_SCALE)).then_inc(S["h3_sb_ok"], 1)

            for g in range(GROUPS):
                act.wait_ge(S["u_ps"], g + 1)
                freed(act, "h2_ps", g)
                act.activation(hid1T[0:F1, :], ps_u, ACT.Relu, scale=H_SCALE / Z_SCALE).then_inc(S["h1_ok"], 1)
                act.wait_ge(S["h2_ps"], g + 1)
                freed(act, "h3_ps", g)
                act.activation(hid2T[0:3 * F2, :], ps_h2[0:3 * F2, :], ACT.Relu).then_inc(S["h2_hi"], 1)
                if g > 0:
                    h3_rows(g - 1)
            deviations(BATCHES_2[0], "aggr2", "std2_ok")
            h3_rows(GROUPS - 1)
            for g in range(GROUPS):
                group = slice(g * GROUP, (g + 1) * GROUP)
                copy_transposed(g, xn2T[g % 2], ("xn2T_ps", "xn2T_sb", "gates_ps"), 2)
                if g == 1:
                    deviations(BATCHES_2[1], "aggr2", "std2_ok")
                act.activation(x_tab[:, group, 0:D], xs[:, group, :], ACT.Copy, scale=X_SCALE).then_inc(S["x_hi"], 1)
            act.wait_ge(S["exp_in"], 1)
            act.activation(ex, dlt, ACT.Exp).then_inc(S["exp_ok"], 1)
            act.wait_ge(S["table_loaded"], 1)
            load_table(ACT.Gelu)

            def gelu(t):
                act.wait_ge(S["hb_ok"], t + 1)
                freed(act, "hT_ps", t)
                act.activation(hid32, hb, ACT.Gelu).then_inc(S["gelu_ok"], 1)

            def high_half(t):
                act.wait_ge(S["hT_ps"], t + 1)
                act.activation(hT_hi, ps_hT, ACT.Copy, scale=H_SCALE).then_inc(S["hT_hi_ok"], 1)

            def weigh(t):
                act.wait_ge(S["y_a_ok"], t + 1)
                freed(act, "y_scattered", 16 * t)
                act.activation(y_b, y_a, ACT.Copy, scale=slot_gate[:, bass.ds(t, 1)]).then_inc(S["y_ok"], 1)

            act.wait_ge(S["x_stored"], 16 * GROUPS)
            gelu(0)
            for t in peeled(act, SLOT_TILES - 1):
                high_half(t)
                gelu(t + 1)
                weigh(t)
            high_half(SLOT_TILES - 1)
            weigh(SLOT_TILES - 1)

        @block.tensor
        def _(pe):
            def keep_busy(n):
                with pe.Fori(0, n) as _i:
                    pe.matmul(ps_idle, zero16[:, 0:P], zeros_wide(BANK), start=True, stop=True)

            pe.wait_ge(S["zeros"], 4)
            keep_busy(26)
            pe.wait_ge(S["consts"], 1)

            def transposes(g, rows, names, banks=range(GROUP)):
                n_rows, n_ps, n_sb = names
                for j in banks:
                    pe.wait_ge(S[n_rows], GROUP * g + (j + 1))
                    freed(pe, n_sb, GROUP * g + (j + 1 - GROUP))
                    for c in range(2):
                        last = pe.transpose(ps_t[j][:, c * P:(c + 1) * P], rows[:, j, c * P:(c + 1) * P], ident[:, :])
                    last.then_inc(S[n_ps], 1)

            def z_product(g):
                freed(pe, "z_lo", g - 1)
                for j in range(GROUP):
                    pe.wait_ge(S["xnT_sb"], GROUP * g + (j + 1))
                    for c in range(2):
                        last = pe.matmul(ps_z[g % 2][:, j * F1:(j + 1) * F1], xnT[g % 2][:, j, c * P:(c + 1) * P],
                                         w1g[:, c, :], start=c == 0, stop=c == 1)
                last.then_inc(S["z_ps"], 1)

            transposes(0, xn, ("xn_ok", "xnT_ps", "xnT_sb"))
            pe.wait_ge(S["params_in"], 16 * PARAMS)
            for g in range(GROUPS - 1):
                transposes(g + 1, xn, ("xn_ok", "xnT_ps", "xnT_sb"))
                z_product(g)
            z_product(GROUPS - 1)

            banks = [(a, min(a + BANK, NODES)) for a in range(0, NODES, BANK)]
            pe.wait_ge(S["zeros"], 4)
            pe.wait_ge(S["z_lo"], GROUPS)
            for a, b in banks:
                last = pe.matmul(ps_agg[:, a:b], zero16[:, 0:P], zeros_wide(b - a), start=True, stop=False,
                                 skip_group_check=True)
            last.then_inc(S["edge_done"], UNROLL)
            with pe.Fori(0, EDGE_LOOPS) as i:
                for j in range(UNROLL):
                    pe.wait_ge(z_in[j], 16 * i + 16)
                    pe.wait_ge(S["hot_ok"], UNROLL * i + (j + 1))
                    for a, b in banks:
                        last = pe.matmul(ps_agg[:, a:b], z_rows[:, j, :], hot[:, j % HOT_RING, a:b],
                                         start=False, stop=False, skip_group_check=True)
                    last.then_inc(S["edge_done"], 1)
            for a, b in banks:
                last = pe.matmul(ps_agg[:, a:b], zero16[:, 0:P], zeros_wide(b - a), start=False, stop=True,
                                 skip_group_check=True)
            last.then_inc(S["edge_done"], 1)

            pe.wait_ge(S["wident_ok"], 1)
            pe.wait_ge(S["w3_ok"], 1)
            pe.wait_ge(S["agg_copied"], 3)
            def fold_halves(g):
                freed(pe, "h1_ok", g)
                pe.wait_ge(S["z_now_ok"], g + 1)
                for j in range(GROUP):
                    pe.matmul(ps_u[:, j * P:(j + 1) * P], fold[:, :], agg_sb[:, bass.ds(g * GROUP * P + j * P, P)],
                              start=True, stop=False)
                    last = pe.matmul(ps_u[:, j * P:(j + 1) * P], z_now[:, j, :], w_ident[:, :], start=False, stop=True)
                last.then_inc(S["u_ps"], 1)

            def middle(g):
                pe.wait_ge(S["h1_ok"], g + 1)
                freed(pe, "h2_ok", g)
                pe.matmul(ps_h2[:, 0:BANK], w2g[:, :], hid1T[0:F1, 0:BANK], start=True, stop=True)
                pe.matmul(ps_h2[:, BANK:], w2g[:, :], hid1T[0:F1, BANK:], start=True, stop=True).then_inc(S["h2_ps"], 1)

            def widen(g):
                pe.wait_ge(S["h2_ok"], g + 1)
                freed(pe, "h3_sb_ok", g)
                for j in range(GROUP):
                    last = pe.matmul(ps_h3[:, j * D:(j + 1) * D], hid2T[0:3 * F2, j * P:(j + 1) * P], w3_parts[:, :],
                                     start=True, stop=True)
                last.then_inc(S["h3_ps"], 1)

            fold_halves(0)
            for g in peeled(pe, GROUPS - 1):
                middle(g)
                fold_halves(g + 1)
                widen(g)
            middle(GROUPS - 1)
            widen(GROUPS - 1)

            rows_of = lambda g: xs[:, g * GROUP:(g + 1) * GROUP, :]
            names2 = ("xn2_ok", "xn2T_ps", "xn2T_sb")

            def gates(g):
                for j in range(GROUP):
                    at = (g * GROUP + j) * EXPERTS
                    pe.wait_ge(S["xn2T_sb"], GROUP * g + (j + 1))
                    for c in range(2):
                        last = pe.matmul(ps_gate[:, at:at + EXPERTS], xn2T[g % 2][:, j, c * P:(c + 1) * P], wgate[:, c, :],
                                         start=c == 0, stop=c == 1)
                last.then_inc(S["gates_ps"], 1)

            pe.wait_ge(S["h2_ok"], GROUPS)
            transposes(0, rows_of(0), names2, range(GROUP - 1))
            pe.wait_ge(S["h3_sb_ok"], GROUPS)
            transposes(0, rows_of(0), names2, range(GROUP - 1, GROUP))
            for g in range(GROUPS):
                if g + 1 < GROUPS:
                    transposes(g + 1, rows_of(g + 1), names2)
                gates(g)
                if g + 1 < GROUPS:
                    keep_busy(6)

            pe.wait_ge(S["counts_in"], 1)
            pe.wait_ge(S["const2"], 4)
            pe.matmul(ps_count[:, 0:TE], before, tmp, start=True, stop=True)
            pe.matmul(ps_count[:, TE:], ones, tmp, start=True, stop=True).then_inc(S["counts_ps"], 1)
            pe.matmul(ps_slot, zero16[:, 0:P], zeros_wide(2 * SLOT_TILES), start=True, stop=False,
                      skip_group_check=True).then_inc(S["pair_done"], 2)
            with pe.Fori(0, TOPK * TILES // (2 * SLOT_COLS)) as i:
                for s in range(2):
                    pe.wait_ge(S["lo_hot_ok"], 2 * i + (s + 1))
                    pe.wait_ge(S["values_ok"], 4 * i + 2 * (s + 3))
                    for c in range(SLOT_COLS):
                        last = pe.matmul(ps_slot, lo_hot[:, s, c, :], val_hi[:, s, c].rearrange("p v n -> p (v n)"),
                                         start=False, stop=False, skip_group_check=True)
                    last.then_inc(S["pair_done"], 1)
            pe.matmul(ps_slot, zero16[:, 0:P], zeros_wide(2 * SLOT_TILES), start=False, stop=True,
                      skip_group_check=True).then_inc(S["slots_ps"], 1)

            def transpose_tokens(t):
                pe.wait_ge(S["tok_gathered"], 16 * t + 16)
                freed(pe, "tok_sb", t)
                for c in range(4):
                    last = pe.transpose(ps_xT[:, c * P:(c + 1) * P], x_rows[:, c * P:(c + 1) * P], ident16[:, :])
                last.then_inc(S["tok_ps"], 1)

            def first_product(t):
                base = pe.value_load(tile_base[0:1, bass.ds(t, 1)], min_val=0, max_val=(EXPERTS - 1) * 2 * HID)
                pe.wait_ge(S["tok_sb"], t + 1)
                freed(pe, "hb_ok", t)
                for half in range(2):
                    o = ps_hid[:, half * BANK:(half + 1) * BANK]
                    for c in range(2):
                        at = bass.ds(base + (c * HID + half * BANK), BANK)
                        pe.matmul(o, xT[:, c * P:(c + 1) * P], w_hi[:, at], start=c == 0, stop=False)
                        pe.matmul(o, xT[:, (2 + c) * P:(3 + c) * P], w_hi[:, at], start=False, stop=False)
                        last = pe.matmul(o, xT[:, c * P:(c + 1) * P], w_lo[:, at], start=False, stop=c == 1)
                last.then_inc(S["hid_ps"], 1)

            def transpose_hidden(t):
                pe.wait_ge(S["gelu_ok"], t + 1)
                freed(pe, "hT_lo_ok", t)
                for m in range(HID // P):
                    last = pe.transpose(ps_hT[:, m * P:(m + 1) * P], hid32[:, m * P:(m + 1) * P], ident[:, :])
                last.then_inc(S["hT_ps"], 1)

            def second_product(t):
                base = pe.value_load(tile_base[0:1, bass.ds(t, 1)], min_val=0, max_val=(EXPERTS - 1) * 2 * HID)
                pe.wait_ge(S["hT_lo_ok"], t + 1)
                freed(pe, "y_a_ok", t)
                n = HID // P
                for m in range(n):
                    at = bass.ds(base + (CHUNKS // 2 * CHUNK + m * D), D)
                    pe.matmul(ps_y, hT_hi[:, m * P:(m + 1) * P], w_hi[:, at], start=m == 0, stop=False)
                    pe.matmul(ps_y, hT_lo[:, m * P:(m + 1) * P], w_hi[:, at], start=False, stop=False)
                    last = pe.matmul(ps_y, hT_hi[:, m * P:(m + 1) * P], w_lo[:, at], start=False, stop=m == n - 1)
                last.then_inc(S["y_ps"], 1)

            pe.wait_ge(S["tables_ok"], 1)
            pe.wait_ge(S["w_lo_ok"], 2 * CHUNKS)
            transpose_tokens(0)
            first_product(0)
            transpose_tokens(1)
            for t in peeled(pe, SLOT_TILES - 2):
                transpose_hidden(t)
                first_product(t + 1)
                transpose_tokens(t + 2)
                second_product(t)
            transpose_hidden(SLOT_TILES - 2)
            first_product(SLOT_TILES - 1)
            second_product(SLOT_TILES - 2)
            transpose_hidden(SLOT_TILES - 1)
            second_product(SLOT_TILES - 1)


def kernel(**inputs):
    import numpy as np
    import concourse.bacc as bacc
    from concourse.bass_utils import run_bass_kernel_spmd

    def grab(name):
        return np.ascontiguousarray(np.asarray(inputs[name]))

    def edges(name, fill):
        a = np.full((P * EDGE_TILES,), fill, np.int32)
        a[:EDGES] = grab(name)
        return a.reshape(P, EDGE_TILES)

    arrays = {
        "x": grab("x"),
        "src": edges("src", -1),
        "dst": edges("dst", 0),
        "w": grab("L0_gnn_w"),
        "w1gT": np.ascontiguousarray(grab("L0_gnn_W1").T),
        "w2gT": np.ascontiguousarray(grab("L0_gnn_W2").T),
        "w3gT": np.ascontiguousarray(grab("L0_gnn_W3").T),
        "wg": grab("L0_ffn_Wg"),
        "bg": grab("L0_ffn_bg"),
        "weights": np.concatenate([
            grab("L0_ffn_W1").reshape(-1, 1024),
            grab("L0_ffn_W2").reshape(EXPERTS, 2, 4, P, D).transpose(0, 1, 3, 2, 4).reshape(-1, 1024)]),
        "b1": grab("L0_ffn_b1").reshape(-1),
        "b2": grab("L0_ffn_b2").reshape(-1),
    }
    nc = bacc.Bacc("TRN2", target_bir_lowering=False, num_devices=1)
    args = [nc.dram_tensor(f"in_{n}", a.shape, mybir.dt.from_np(a.dtype), kind="ExternalInput").ap()
            for n, a in arrays.items()]
    out = nc.dram_tensor("out_0", (NODES, D), mybir.dt.float32, kind="ExternalOutput").ap()
    gnn_moe(nc, *args, out)
    r = run_bass_kernel_spmd(nc, [{f"in_{n}": a for n, a in arrays.items()}], core_ids=[0])
    return r.results[0]["out_0"]
```
